# Optimizing a Trainium2 kernel written in Bass

```python
import numpy as np
import jax
import jax.numpy as jnp

def _softmax(x, axis=-1):
    return jax.nn.softmax(x, axis=axis)

def _gelu(x):
    return jax.nn.gelu(x, approximate=True)

def _silu(x):
    return jax.nn.silu(x)

def _sigmoid(x):
    return jax.nn.sigmoid(x)

def _layernorm(x, axis=-1, eps=1e-05):
    m = jnp.mean(x, axis=axis, keepdims=True)
    v = jnp.var(x, axis=axis, keepdims=True)
    return (x - m) / jnp.sqrt(v + eps)

def _scatter_add(tgt, idx, src, axis=0):
    return tgt.at[idx].add(src)

def _segment_sum(src, seg, n):
    return jax.ops.segment_sum(src, seg, n)
kernel_name = 'mk_macaron_d2_jaxref_r8_81687f'

def setup_inputs(seed: int=0):
    np.random.seed(seed)
    _w = jnp.asarray

    def _L0_attn_setup():
        import jax, jax.numpy as jnp
        import numpy as np
        D_MODEL = 128
        NUM_HEADS = 16
        HEAD_DIM = D_MODEL // NUM_HEADS
        WINDOW = 128
        SCALE = HEAD_DIM ** (-0.5)
        key = jax.random.key(seed)
        ks = jax.random.split(key, 5)
        B, S = (2, 256)
        x = jax.random.normal(ks[0], (B, S, D_MODEL), dtype=jnp.float32)
        init = lambda k: jax.random.normal(k, (D_MODEL, D_MODEL), dtype=jnp.float32) * D_MODEL ** (-0.5)
        return {'x': x, 'Wq': init(ks[1]), 'Wk': init(ks[2]), 'Wv': init(ks[3]), 'Wo': init(ks[4])}
    _L0_attn_in = _L0_attn_setup()

    def _L0_ffn_setup():
        import jax, jax.numpy as jnp
        import numpy as np
        IN_DIM = 128
        OUT_DIM = 128
        NUM_EXPERTS = 8
        TOP_K = 2
        key = jax.random.key(seed)
        ks = jax.random.split(key, 5)
        s = 1.0 / np.sqrt(IN_DIM)
        x = jax.random.normal(ks[0], (4, 256, IN_DIM), dtype=jnp.float32)
        Wg = jax.random.uniform(ks[1], (IN_DIM, NUM_EXPERTS), jnp.float32, -s, s)
        bg = jnp.zeros((NUM_EXPERTS,), jnp.float32)
        We = jax.random.uniform(ks[2], (NUM_EXPERTS, OUT_DIM, IN_DIM), jnp.float32, -s, s)
        be = jax.random.uniform(ks[3], (NUM_EXPERTS, OUT_DIM), jnp.float32, -s, s)
        return {'x': x, 'Wg': Wg, 'bg': bg, 'We': We, 'be': be}
    _L0_ffn_in = _L0_ffn_setup()

    def _L1_attn_setup():
        import jax, jax.numpy as jnp
        import numpy as np
        B, L, D, H, W = (2, 512, 128, 16, 128)
        E = D // H

        def _ln(x, g, b):
            m = jnp.mean(x, axis=-1, keepdims=True)
            v = jnp.mean((x - m) ** 2, axis=-1, keepdims=True)
            return (x - m) / jnp.sqrt(v + 1e-05) * g + b

        def _swa(xn, Wqkv, bqkv, Wp, bp):
            b_, l_, d_ = xn.shape
            nb = l_ // W
            qkv = xn @ Wqkv + bqkv
            q, k, v = jnp.split(qkv, 3, axis=-1)

            def heads(t):
                return t.reshape(b_, l_, H, E).transpose(0, 2, 1, 3)
            q, k, v = (heads(q), heads(k), heads(v))

            def blk(t):
                return t.reshape(b_, H, nb, W, E)
            qb, kb, vb = (blk(q), blk(k), blk(v))
            kprev = jnp.pad(kb, ((0, 0), (0, 0), (1, 0), (0, 0), (0, 0)))[:, :, :nb]
            vprev = jnp.pad(vb, ((0, 0), (0, 0), (1, 0), (0, 0), (0, 0)))[:, :, :nb]
            kc = jnp.concatenate([kprev, kb], axis=3)
            vc = jnp.concatenate([vprev, vb], axis=3)
            scores = jnp.einsum('bhnre,bhnse->bhnrs', qb, kc) / np.float32(np.sqrt(E))
            r = jnp.arange(W)[:, None]
            s = jnp.arange(2 * W)[None, :]
            band = (s >= r + 1) & (s <= r + W)
            first = band & (s >= W)
            mask = jnp.concatenate([first[None], jnp.broadcast_to(band, (nb - 1, W, 2 * W))], axis=0)
            scores = jnp.where(mask[None, None], scores, jnp.float32(-1e+30))
            attn = jax.nn.softmax(scores, axis=-1)
            out = jnp.einsum('bhnrs,bhnse->bhnre', attn, vc)
            out = out.reshape(b_, H, l_, E).transpose(0, 2, 1, 3).reshape(b_, l_, d_)
            return out @ Wp + bp

        def _linattn(xn, Wqkv, bqkv, Wo, bo):
            b_, l_, d_ = xn.shape
            C = 128
            nc = l_ // C
            qkv = xn @ Wqkv + bqkv
            q, k, v = jnp.split(qkv, 3, axis=-1)
            q = q.reshape(b_, l_, H, E)
            k = k.reshape(b_, l_, H, E)
            v = v.reshape(b_, l_, H, E)
            q = jax.nn.elu(q * np.float32(E ** (-0.5))) + np.float32(1.0001)
            k = jax.nn.elu(k) + np.float32(1.0001)

            def chunks(t):
                return t.reshape(b_, nc, C, H, E).transpose(1, 0, 3, 2, 4)
            qc, kc, vc = (chunks(q), chunks(k), chunks(v))
            tril = jnp.tril(jnp.ones((C, C), jnp.float32))

            def step(carry, inp):
                S, z = carry
                qi, ki, vi = inp
                A = jnp.einsum('bhce,bhde->bhcd', qi, ki) * tril
                num = jnp.einsum('bhce,bhef->bhcf', qi, S) + jnp.einsum('bhcd,bhdf->bhcf', A, vi)
                den = jnp.einsum('bhce,bhe->bhc', qi, z) + A.sum(-1)
                o = num / (den[..., None] + 1e-06)
                S = S + jnp.einsum('bhce,bhcf->bhef', ki, vi)
                z = z + ki.sum(2)
                return ((S, z), o)
            S0 = jnp.zeros((b_, H, E, E), jnp.float32)
            z0 = jnp.zeros((b_, H, E), jnp.float32)
            _, out = jax.lax.scan(step, (S0, z0), (qc, kc, vc))
            out = out.transpose(1, 0, 3, 2, 4).reshape(b_, l_, d_)
            return out @ Wo + bo
        key = jax.random.key(seed)
        ks = jax.random.split(key, 9)

        def w(k, shape, s=0.02):
            return jax.random.normal(k, shape, jnp.float32) * s
        return {'x': jax.random.normal(ks[0], (B, L, D), jnp.float32), 'g1': jnp.ones((D,), jnp.float32), 'b1': jnp.zeros((D,), jnp.float32), 'Wqkv_a': w(ks[1], (D, 3 * D)), 'bqkv_a': jnp.zeros((3 * D,), jnp.float32), 'Wp_a': w(ks[2], (D, D)), 'bp_a': jnp.zeros((D,), jnp.float32), 'Wqkv_s': w(ks[3], (D, 3 * D)), 'bqkv_s': jnp.zeros((3 * D,), jnp.float32), 'Wo_s': w(ks[4], (D, D)), 'bo_s': jnp.zeros((D,), jnp.float32), 'Wo': w(ks[5], (D, D)), 'bo': jnp.zeros((D,), jnp.float32), 'gm': jnp.ones((D,), jnp.float32), 'bm': jnp.zeros((D,), jnp.float32), 'W1': w(ks[6], (D, 4 * D)), 'b1m': jnp.zeros((4 * D,), jnp.float32), 'W2': w(ks[7], (4 * D, D)), 'b2m': jnp.zeros((D,), jnp.float32)}
    _L1_attn_in = _L1_attn_setup()

    def _L1_ffn_setup():
        import jax, jax.numpy as jnp
        import numpy as np
        from math import ceil
        CAPACITY_FACTOR = 2.0
        MIN_CAPACITY = 4
        key = jax.random.key(seed)
        ks = jax.random.split(key, 4)
        B, S, D, Di, E = (4, 256, 128, 512, 8)
        x = jax.random.normal(ks[0], (B, S, D), dtype=jnp.float32)
        Wr = jax.random.normal(ks[1], (D, E), dtype=jnp.float32) * D ** (-0.5)
        W1 = jax.random.normal(ks[2], (E, D, Di), dtype=jnp.float32) * D ** (-0.5)
        b1 = jnp.zeros((E, Di), dtype=jnp.float32)
        W2 = jax.random.normal(ks[3], (E, Di, D), dtype=jnp.float32) * Di ** (-0.5)
        b2 = jnp.zeros((E, D), dtype=jnp.float32)
        return {'x': x, 'Wr': Wr, 'W1': W1, 'b1': b1, 'W2': W2, 'b2': b2}
    _L1_ffn_in = _L1_ffn_setup()
    _d = {'L0_attn_x': _L0_attn_in['x'], 'L0_attn_Wq': _L0_attn_in['Wq'], 'L0_attn_Wk': _L0_attn_in['Wk'], 'L0_attn_Wv': _L0_attn_in['Wv'], 'L0_attn_Wo': _L0_attn_in['Wo'], 'L0_ffn_Wg': _L0_ffn_in['Wg'], 'L0_ffn_bg': _L0_ffn_in['bg'], 'L0_ffn_We': _L0_ffn_in['We'], 'L0_ffn_be': _L0_ffn_in['be'], 'L1_attn_g1': _L1_attn_in['g1'], 'L1_attn_b1': _L1_attn_in['b1'], 'L1_attn_Wqkv_a': _L1_attn_in['Wqkv_a'], 'L1_attn_bqkv_a': _L1_attn_in['bqkv_a'], 'L1_attn_Wp_a': _L1_attn_in['Wp_a'], 'L1_attn_bp_a': _L1_attn_in['bp_a'], 'L1_attn_Wqkv_s': _L1_attn_in['Wqkv_s'], 'L1_attn_bqkv_s': _L1_attn_in['bqkv_s'], 'L1_attn_Wo_s': _L1_attn_in['Wo_s'], 'L1_attn_bo_s': _L1_attn_in['bo_s'], 'L1_attn_Wo': _L1_attn_in['Wo'], 'L1_attn_bo': _L1_attn_in['bo'], 'L1_attn_gm': _L1_attn_in['gm'], 'L1_attn_bm': _L1_attn_in['bm'], 'L1_attn_W1': _L1_attn_in['W1'], 'L1_attn_b1m': _L1_attn_in['b1m'], 'L1_attn_W2': _L1_attn_in['W2'], 'L1_attn_b2m': _L1_attn_in['b2m'], 'L1_ffn_Wr': _L1_ffn_in['Wr'], 'L1_ffn_W1': _L1_ffn_in['W1'], 'L1_ffn_b1': _L1_ffn_in['b1'], 'L1_ffn_W2': _L1_ffn_in['W2'], 'L1_ffn_b2': _L1_ffn_in['b2']}
    _x0 = _d['L0_attn_x']
    _d['L0_attn_x'] = jax.random.normal(jax.random.fold_in(jax.random.key(seed), 1), (8, 512, 128), dtype=_x0.dtype)
    del _x0
    return _d

def reference(L0_attn_x, L0_attn_Wq, L0_attn_Wk, L0_attn_Wv, L0_attn_Wo, L0_ffn_Wg, L0_ffn_bg, L0_ffn_We, L0_ffn_be, L1_attn_g1, L1_attn_b1, L1_attn_Wqkv_a, L1_attn_bqkv_a, L1_attn_Wp_a, L1_attn_bp_a, L1_attn_Wqkv_s, L1_attn_bqkv_s, L1_attn_Wo_s, L1_attn_bo_s, L1_attn_Wo, L1_attn_bo, L1_attn_gm, L1_attn_bm, L1_attn_W1, L1_attn_b1m, L1_attn_W2, L1_attn_b2m, L1_ffn_Wr, L1_ffn_W1, L1_ffn_b1, L1_ffn_W2, L1_ffn_b2):

    def _L0_attn_ref(x, Wq, Wk, Wv, Wo):
        import jax, jax.numpy as jnp
        import numpy as np
        D_MODEL = 128
        NUM_HEADS = 16
        HEAD_DIM = D_MODEL // NUM_HEADS
        WINDOW = 128
        SCALE = HEAD_DIM ** (-0.5)
        B, S, _ = x.shape

        def heads(W):
            return (x @ W.T).reshape(B, S, NUM_HEADS, HEAD_DIM).transpose(0, 2, 1, 3)
        q, k, v = (heads(Wq), heads(Wk), heads(Wv))
        attn = jnp.einsum('bhqd,bhkd->bhqk', q, k) * SCALE
        idx = jnp.arange(S)
        band = jnp.abs(idx[:, None] - idx[None, :]) <= WINDOW
        attn = jnp.where(band[None, None], attn, -jnp.inf)
        attn = jax.nn.softmax(attn, axis=-1)
        out = jnp.einsum('bhqk,bhkd->bhqd', attn, v)
        out = out.transpose(0, 2, 1, 3).reshape(B, S, D_MODEL)
        return out @ Wo.T

    def _L0_ffn_ref(x, Wg, bg, We, be):
        import jax, jax.numpy as jnp
        import numpy as np
        IN_DIM = 128
        OUT_DIM = 128
        NUM_EXPERTS = 8
        TOP_K = 2
        gate = jax.nn.softmax(x @ Wg + bg, axis=-1)
        topk_vals, topk_idx = jax.lax.top_k(gate, TOP_K)
        onehot = jax.nn.one_hot(topk_idx, NUM_EXPERTS, dtype=gate.dtype)
        gate_sparse = jnp.einsum('bsk,bske->bse', topk_vals, onehot)
        gate_sparse = gate_sparse / jnp.sum(gate_sparse, axis=-1, keepdims=True)
        y = jnp.einsum('bsi,eoi->bseo', x, We) + be[None, None, :, :].transpose(0, 1, 2, 3)
        out = jnp.einsum('bseo,bse->bso', y, gate_sparse)
        return out

    def _L1_attn_ref(x, g1, b1, Wqkv_a, bqkv_a, Wp_a, bp_a, Wqkv_s, bqkv_s, Wo_s, bo_s, Wo, bo, gm, bm, W1, b1m, W2, b2m):
        import jax, jax.numpy as jnp
        import numpy as np
        B, L, D, H, W = (2, 512, 128, 16, 128)
        E = D // H

        def _ln(x, g, b):
            m = jnp.mean(x, axis=-1, keepdims=True)
            v = jnp.mean((x - m) ** 2, axis=-1, keepdims=True)
            return (x - m) / jnp.sqrt(v + 1e-05) * g + b

        def _swa(xn, Wqkv, bqkv, Wp, bp):
            b_, l_, d_ = xn.shape
            nb = l_ // W
            qkv = xn @ Wqkv + bqkv
            q, k, v = jnp.split(qkv, 3, axis=-1)

            def heads(t):
                return t.reshape(b_, l_, H, E).transpose(0, 2, 1, 3)
            q, k, v = (heads(q), heads(k), heads(v))

            def blk(t):
                return t.reshape(b_, H, nb, W, E)
            qb, kb, vb = (blk(q), blk(k), blk(v))
            kprev = jnp.pad(kb, ((0, 0), (0, 0), (1, 0), (0, 0), (0, 0)))[:, :, :nb]
            vprev = jnp.pad(vb, ((0, 0), (0, 0), (1, 0), (0, 0), (0, 0)))[:, :, :nb]
            kc = jnp.concatenate([kprev, kb], axis=3)
            vc = jnp.concatenate([vprev, vb], axis=3)
            scores = jnp.einsum('bhnre,bhnse->bhnrs', qb, kc) / np.float32(np.sqrt(E))
            r = jnp.arange(W)[:, None]
            s = jnp.arange(2 * W)[None, :]
            band = (s >= r + 1) & (s <= r + W)
            first = band & (s >= W)
            mask = jnp.concatenate([first[None], jnp.broadcast_to(band, (nb - 1, W, 2 * W))], axis=0)
            scores = jnp.where(mask[None, None], scores, jnp.float32(-1e+30))
            attn = jax.nn.softmax(scores, axis=-1)
            out = jnp.einsum('bhnrs,bhnse->bhnre', attn, vc)
            out = out.reshape(b_, H, l_, E).transpose(0, 2, 1, 3).reshape(b_, l_, d_)
            return out @ Wp + bp

        def _linattn(xn, Wqkv, bqkv, Wo, bo):
            b_, l_, d_ = xn.shape
            C = 128
            nc = l_ // C
            qkv = xn @ Wqkv + bqkv
            q, k, v = jnp.split(qkv, 3, axis=-1)
            q = q.reshape(b_, l_, H, E)
            k = k.reshape(b_, l_, H, E)
            v = v.reshape(b_, l_, H, E)
            q = jax.nn.elu(q * np.float32(E ** (-0.5))) + np.float32(1.0001)
            k = jax.nn.elu(k) + np.float32(1.0001)

            def chunks(t):
                return t.reshape(b_, nc, C, H, E).transpose(1, 0, 3, 2, 4)
            qc, kc, vc = (chunks(q), chunks(k), chunks(v))
            tril = jnp.tril(jnp.ones((C, C), jnp.float32))

            def step(carry, inp):
                S, z = carry
                qi, ki, vi = inp
                A = jnp.einsum('bhce,bhde->bhcd', qi, ki) * tril
                num = jnp.einsum('bhce,bhef->bhcf', qi, S) + jnp.einsum('bhcd,bhdf->bhcf', A, vi)
                den = jnp.einsum('bhce,bhe->bhc', qi, z) + A.sum(-1)
                o = num / (den[..., None] + 1e-06)
                S = S + jnp.einsum('bhce,bhcf->bhef', ki, vi)
                z = z + ki.sum(2)
                return ((S, z), o)
            S0 = jnp.zeros((b_, H, E, E), jnp.float32)
            z0 = jnp.zeros((b_, H, E), jnp.float32)
            _, out = jax.lax.scan(step, (S0, z0), (qc, kc, vc))
            out = out.transpose(1, 0, 3, 2, 4).reshape(b_, l_, d_)
            return out @ Wo + bo
        xn = _ln(x, g1, b1)
        attn_out = _swa(xn, Wqkv_a, bqkv_a, Wp_a, bp_a)
        ssm_out = _linattn(xn, Wqkv_s, bqkv_s, Wo_s, bo_s)
        mixed = (attn_out + ssm_out) @ Wo + bo
        x1 = x + mixed
        h = _ln(x1, gm, bm)
        mlp = jax.nn.gelu(h @ W1 + b1m, approximate=False) @ W2 + b2m
        return x1 + mlp

    def _L1_ffn_ref(x, Wr, W1, b1, W2, b2):
        import jax, jax.numpy as jnp
        import numpy as np
        from math import ceil
        CAPACITY_FACTOR = 2.0
        MIN_CAPACITY = 4
        B, S, D = x.shape
        E = Wr.shape[1]
        N = B * S
        k = max(MIN_CAPACITY, ceil(N * CAPACITY_FACTOR / E))
        xt = x.reshape(N, D)
        scores = jax.nn.softmax(xt @ Wr, axis=-1)
        G, idx = jax.lax.top_k(scores.T, k)
        X_in = xt[idx]
        h = jax.nn.gelu(jnp.einsum('ekd,edh->ekh', X_in, W1) + b1[:, None, :], approximate=False)
        X_e = jnp.einsum('ekh,ehd->ekd', h, W2) + b2[:, None, :]
        contrib = (G[..., None] * X_e).reshape(E * k, D)
        out = jnp.zeros((N, D), dtype=x.dtype).at[idx.reshape(-1)].add(contrib)
        return out.reshape(B, S, D)
    x = L0_attn_x
    x = x + 0.5 * _L0_ffn_ref(_layernorm(x, axis=-1), L0_ffn_Wg, L0_ffn_bg, L0_ffn_We, L0_ffn_be)
    x = x + _L0_attn_ref(_layernorm(x, axis=-1), L0_attn_Wq, L0_attn_Wk, L0_attn_Wv, L0_attn_Wo)
    x = x + 0.5 * _L0_ffn_ref(_layernorm(x, axis=-1), L0_ffn_Wg, L0_ffn_bg, L0_ffn_We, L0_ffn_be)
    x = x + 0.5 * _L1_ffn_ref(_layernorm(x, axis=-1), L1_ffn_Wr, L1_ffn_W1, L1_ffn_b1, L1_ffn_W2, L1_ffn_b2)
    x = x + _L1_attn_ref(_layernorm(x, axis=-1), L1_attn_g1, L1_attn_b1, L1_attn_Wqkv_a, L1_attn_bqkv_a, L1_attn_Wp_a, L1_attn_bp_a, L1_attn_Wqkv_s, L1_attn_bqkv_s, L1_attn_Wo_s, L1_attn_bo_s, L1_attn_Wo, L1_attn_bo, L1_attn_gm, L1_attn_bm, L1_attn_W1, L1_attn_b1m, L1_attn_W2, L1_attn_b2m)
    x = x + 0.5 * _L1_ffn_ref(_layernorm(x, axis=-1), L1_ffn_Wr, L1_ffn_W1, L1_ffn_b1, L1_ffn_W2, L1_ffn_b2)
    return x

_drawn_inputs = setup_inputs


def setup_inputs(seed=0):
    import zlib

    import numpy as np

    out = dict(_drawn_inputs(seed))
    spreads = {'L0_ffn_bg': (0.0, 0.1),
     'L1_attn_g1': (1.0, 0.6),
     'L1_attn_b1': (0.0, 0.8),
     'L1_attn_bqkv_a': (0.0, 0.8),
     'L1_attn_bp_a': (0.0, 0.709),
     'L1_attn_bqkv_s': (0.0, 0.8),
     'L1_attn_bo_s': (0.0, 0.698),
     'L1_attn_bo': (0.0, 0.505),
     'L1_attn_gm': (1.0, 0.6),
     'L1_attn_bm': (0.0, 2.0),
     'L1_attn_b1m': (0.0, 0.645),
     'L1_attn_b2m': (0.0, 0.491),
     'L1_ffn_b1': (0.0, 0.371),
     'L1_ffn_b2': (0.0, 0.1)}
    factors = {'L1_attn_Wqkv_a': 8.0,
     'L1_attn_Wp_a': 8.0,
     'L1_attn_Wqkv_s': 8.0,
     'L1_attn_Wo_s': 8.0,
     'L1_attn_Wo': 3.337,
     'L1_attn_W1': 2.981}
    for name, (base, spread) in spreads.items():
        noise = np.random.default_rng([zlib.crc32(name.encode()), seed]).standard_normal(out[name].shape)
        drawn = base * np.exp(spread * noise) if base else spread * noise
        out[name] = jnp.asarray(drawn.astype(out[name].dtype))
    for name, factor in factors.items():
        out[name] = (out[name] * factor).astype(out[name].dtype)
    return out
```

```python
from contextlib import ExitStack

import concourse.bass as bass
from concourse import mybir

F32 = mybir.dt.float32
BF16 = mybir.dt.bfloat16
U32 = mybir.dt.uint32
ALU = mybir.AluOpType
ACT = mybir.ActivationFunctionType
AXX = mybir.AxisListType.X

P = 128
D = 128
SEQ = 512
EPS = 1e-5
BITS = 30


class Chain:

    def __init__(self, eng, sem, base=0):
        self.eng, self.sem, self.base, self.n = eng, sem, base, 0

    def __call__(self, ins):
        ins.then_inc(self.sem, 1)
        self.n += 1
        self.eng.wait_ge(self.sem, self.base + self.n)


class Stage:

    def __init__(self, nc, name):
        self.nc, self.name, self.ctx, self.sems = nc, name, ExitStack(), []

    def __enter__(self):
        return self

    def __exit__(self, *a):
        if a[0] is None and self.sems:
            self.nc.clear_and_free_semaphores(self.sems)
            self.nc.all_engine_barrier()
        self.ctx.close()

    def sb(self, name, shape, dt=F32):
        return self.ctx.enter_context(self.nc.sbuf_tensor(f"{self.name}_{name}", shape, dt))

    def banks(self):
        return self.ctx.enter_context(self.nc.psum_tensor(f"{self.name}_banks", [P, 8, 512], F32))

    def sem(self, name):
        self.sems.append(self.nc.alloc_semaphore(name=f"{self.name}_{name}"))
        return self.sems[-1]


def spread(ap, n, axis):
    shape = list(ap.shape)
    return ap.unsqueeze(axis).broadcast_to(shape[:axis] + [n] + shape[axis:])


def make_constants(nc, C, row_biases):
    n_bias = sum(n for _, n in row_biases)
    with Stage(nc, "const") as st:
        row = st.sb("row", [1, n_bias])
        rest = st.sb("rest", [1, n_bias])
        parts = st.sb("parts", [1, 3, n_bias], BF16)
        s_rows, s_parts, s_moved = st.sem("rows_landed"), st.sem("parts_done"), st.sem("parts_moved")
        s_dve, s_pool, s_bits = st.sem("dve_chain"), st.sem("pool_chain"), st.sem("bits_set")
        with nc.Block() as block:

            @block.sync
            def _(sp):
                at = 0
                for src, n in row_biases:
                    sp.dma_start(row[0:1, at:at + n], src).then_inc(s_rows, 16)
                    at += n
                sp.wait_ge(s_parts, 1)
                for k in range(3):
                    sp.dma_start(C["bias_rows"][k:k + 1, :], parts[0:1, k, :]).then_inc(s_moved, 16)
                sp.wait_ge(s_moved, 48)

            @block.vector
            def _(dve):
                step = Chain(dve, s_dve)
                dve.wait_ge(s_rows, 16 * len(row_biases))
                step(dve.tensor_copy(parts[:, 0, :], row[:, :]))
                step(dve.tensor_tensor(rest[:, :], row[:, :], parts[:, 0, :], ALU.subtract))
                step(dve.tensor_copy(parts[:, 1, :], rest[:, :]))
                dve.tensor_tensor(parts[:, 2, :], rest[:, :], parts[:, 1, :], ALU.subtract).then_inc(s_parts, 1)

            @block.gpsimd
            def _(pool):
                step = Chain(pool, s_pool)
                step(pool.memset(C["ident"][:, :], 0.0))
                step(pool.affine_select(out=C["ident"][:, :], in_=C["ident"][:, :], compare_op=ALU.not_equal,
                                        fill=1.0, base=0, pattern=[[-1, P]], channel_multiplier=1))
                step(pool.tensor_copy(C["ident_bf"][:, :], C["ident"][:, :]))
                step(pool.memset(C["ones_bf"][:, :], 1.0))
                step(pool.affine_select(out=C["upto_bf"][:, :], in_=C["ones_bf"][:, :], compare_op=ALU.is_ge,
                                        fill=0.0, base=0, pattern=[[1, P]], channel_multiplier=-1))
                step(pool.memset(C["zero_bf"][:, :], 0.0))
                for name, pat, mul, base in (("col_ge", 1, -1, 0), ("col_gt", 1, -1, -1), ("col_le", -1, 1, 0),
                                             ("col_lt", -1, 1, -1)):
                    for k in range(4):
                        step(pool.affine_select(out=C[name][:, k, :], in_=C["zero_bf"][:, :], compare_op=ALU.is_ge,
                                                fill=-1e30, base=base, pattern=[[pat, P]],
                                                channel_multiplier=mul))
                for k in range(BITS):
                    pool.memset(C["bit"][:, k, :], float(2 ** (BITS - 1 - k))).then_inc(s_bits, 1)
                pool.wait_ge(s_bits, BITS)
                step(pool.tensor_copy(C["bit_i"][:, :, :], C["bit"][:, :, :]))
                step(pool.iota(C["rank"][:, :], pattern=[[-1, 8]], base=8, channel_multiplier=0,
                               allow_small_or_imprecise_dtypes=True))


def norm_stage(nc, C, name, x, keep_norm=None, norm_to_dram=None, xT_all=None, gain=None, shift=None,
               router=None, logits=None, router_bias=None, x_to_dram=None):
    nt = x.shape[1]
    nch = nt // 4
    half = nt // 2
    with Stage(nc, name) as st:
        ps = st.banks()
        stats = st.sb("stats", [P, nt, 6])
        mv = st.sb("mean_var", [P, nt, 2])
        std = st.sb("std", [P, nt])
        rstd = st.sb("rstd", [P, nt])
        eps = st.sb("eps", [P, 1])
        xn = st.sb("xn", [P, 2, 4, D])
        xTc = st.sb("xT_chunk", [P, 2, SEQ])
        s_stats, s_var, s_std = st.sem("stats"), st.sem("var_ready"), st.sem("std_ready")
        s_dve, s_eps, s_zero = st.sem("dve_chain"), st.sem("eps_ready"), st.sem("logits_zeroed")
        s_xn, s_tp, s_tev, s_lg = st.sem("xn_ready"), st.sem("transposed"), st.sem("xT_ready"), st.sem("logits_ready")
        s_out, s_x = [st.sem("norm_stored_even"), st.sem("norm_stored_odd")], st.sem("x_stored")
        pT = [ps[:, u, :] for u in range(2)]
        pL = ps[:, 2, 0:nt * 8]
        with nc.Block() as block:

            @block.vector
            def _(dve):
                dve.memset(eps[:, :], EPS).then_inc(s_eps, 1)
                if router is not None:
                    dve.memset(pL, 0.0).then_inc(s_zero, 1)
                for h in range(2):
                    for t in range(h * half, (h + 1) * half):
                        dve.bn_stats(stats[:, t, :], x[:, t, :]).then_inc(s_stats, 1)
                    dve.wait_ge(s_stats, (h + 1) * half)
                    for t in range(h * half, (h + 1) * half):
                        dve.bn_aggr(mv[:, t, :], stats[:, t, :]).then_inc(s_var, 1)
                step = Chain(dve, s_dve)
                for h in range(2):
                    own = slice(h * half, (h + 1) * half)
                    dve.wait_ge(s_std, h + 1)
                    step(dve.reciprocal(rstd[:, own], std[:, own]))
                    with dve.Fori(h * nch // 4, (h + 1) * nch // 4) as i:
                        for u in range(2):
                            c = i * 2 + u
                            if keep_norm is None:
                                dve.wait_ge(s_tp, c + 1)
                                if norm_to_dram is not None:
                                    dve.wait_ge(s_out[u], 1 + i * 16)
                            for k in range(4):
                                t = c * 4 + k
                                dst = xn[:, u, k, :] if keep_norm is None else \
                                    keep_norm[:, bass.ds(t, 1), :].rearrange("p a d -> p (a d)")
                                dve.tensor_scalar(dst, x[:, bass.ds(t, 1), :].rearrange("p a d -> p (a d)"),
                                                  mv[:, bass.ds(t, 1), 0:1].rearrange("p a d -> p (a d)"),
                                                  rstd[:, bass.ds(t, 1)],
                                                  ALU.subtract, ALU.mult).then_inc(s_xn, 1)
                if router is not None:
                    dve.wait_ge(s_lg, 2 + nch)
                    src = pL.rearrange("p (t e) -> p t e", e=8)
                    if router_bias is None:
                        dve.tensor_copy(logits[:, :, :], src)
                    else:
                        dve.tensor_tensor(logits[:, :, :], src, spread(router_bias[:, :], nt, 1), ALU.add)

            @block.scalar
            def _(act):
                act.sem_inc(s_tev, 2)
                act.wait_ge(s_eps, 1)
                for h in range(2):
                    act.wait_ge(s_var, (h + 1) * half)
                    act.activation(std[:, h * half:(h + 1) * half], mv[:, h * half:(h + 1) * half, 1], ACT.Sqrt,
                                   bias=eps[:, :]).then_inc(s_std, 1)
                if keep_norm is not None:
                    return
                kw = {}
                if gain is not None:
                    kw = dict(scale=gain, bias=shift)
                fn = ACT.Identity if gain is not None else ACT.Copy
                with act.Fori(0, nch // 2) as i:
                    for u in range(2):
                        c = i * 2 + u
                        act.wait_ge(s_tp, 2 + c + 1)
                        if xT_all is not None:
                            ins = act.activation(xT_all[:, bass.ds(c * SEQ, SEQ)], pT[u], fn, **kw)
                        if router is not None:
                            act.wait_ge(s_lg, c + 1)
                            ins = act.activation(xTc[:, u, :], pT[u], fn, **kw)
                        ins.then_inc(s_tev, 1)

            @block.tensor
            def _(pe):
                pe.sem_inc(s_tp, 2)
                pe.sem_inc(s_lg, 2)
                if keep_norm is not None:
                    return
                if router is not None:
                    pe.wait_ge(s_zero, 1)
                with pe.Fori(0, nch // 2) as i:
                    for u in range(2):
                        c = i * 2 + u
                        pe.wait_ge(s_tev, c + 1)
                        for k in range(4):
                            pe.wait_ge(s_xn, c * 4 + k + 1)
                            mm = pe.transpose(pT[u][:, k * P:(k + 1) * P], xn[:, u, k, :], C["ident"][:, :])
                        mm.then_inc(s_tp, 1)
                    if router is not None:
                        for u in range(2):
                            c = i * 2 + u
                            pe.wait_ge(s_tev, 2 + c + 1)
                            for k in range(4):
                                mm = pe.matmul(ps[:, 2, bass.ds(c * 32 + 8 * k, 8)], xTc[:, u, k * P:(k + 1) * P],
                                               router, start=False, stop=False, skip_group_check=True)
                            mm.then_inc(s_lg, 1)

            @block.sync
            def _(sp):
                for u in range(2):
                    sp.sem_inc(s_out[u], 1)
                if x_to_dram is not None:
                    sp.dma_start(x_to_dram.rearrange("(t p) d -> p t d", p=P), x[:, :, :]).then_inc(s_x, 16)
                if norm_to_dram is not None:
                    rows = norm_to_dram.rearrange("(t p) d -> p t d", p=P)
                    with sp.Fori(0, nch // 2) as i:
                        for u in range(2):
                            c = i * 2 + u
                            sp.wait_ge(s_xn, c * 4 + 4)
                            sp.dma_start(rows[:, bass.ds(c * 4, 4), :], xn[:, u, :, :]).then_inc(s_out[u], 16)
                    for u in range(2):
                        sp.wait_ge(s_out[u], 1 + nch // 2 * 16)
                if x_to_dram is not None:
                    sp.wait_ge(s_x, 16)


def linear_experts(nc, C, name, x, xT_all, logits, We, bias_at):
    nt = x.shape[1]
    E = 8
    with Stage(nc, name) as st:
        ps = st.banks()
        we = st.sb("we", [P, E * D])
        top = st.sb("top", [P, nt])
        ex = st.sb("exps", [P, nt, E])
        w = st.sb("ranked", [P, nt, E])
        wm = st.sb("best_rank", [P, nt])
        hot = st.sb("hot", [P, 2, nt, E])
        gates = st.sb("gates", [P, nt, E])
        xT = st.sb("xT_tile", [P, 4, D])
        s_w, s_exp, s_shift, s_dve = st.sem("weights"), st.sem("exps"), st.sem("shifted"), st.sem("dve_chain")
        s_acc = st.sem("acc_chain")
        s_xT, s_y, s_used = st.sem("xT_ready"), st.sem("y_ready"), st.sem("y_used")
        with nc.Block() as block:

            @block.sync
            def _(sp):
                sp.dma_start(we[:, :], We).then_inc(s_w, 16)

            @block.scalar
            def _(act):
                act.wait_ge(s_shift, 1)
                act.activation(ex[:, :, :], ex[:, :, :], ACT.Exp).then_inc(s_exp, 1)

            @block.gpsimd
            def _(pool):
                with pool.Fori(0, nt // 4) as i:
                    for k in range(4):
                        t = i * 4 + k
                        pool.wait_ge(s_y, t + 1)
                        pool.tensor_copy(xT[:, k, :], xT_all[:, bass.ds(t * P, P)]).then_inc(s_xT, 1)

            @block.tensor
            def _(pe):
                pe.sem_inc(s_y, 4)
                pe.wait_ge(s_w, 16)
                with pe.Fori(0, nt // 4) as i:
                    for k in range(4):
                        t = i * 4 + k
                        pe.wait_ge(s_xT, t + 1)
                        pe.wait_ge(s_used, t + 1)
                        for h in range(2):
                            bank = ps[:, 2 * k + h, :]
                            pe.matmul(bank, C["ones_bf"][0:3, :],
                                      C["bias_rows"][:, bias_at + 512 * h:bias_at + 512 * h + 512],
                                      start=True, stop=False)
                            mm = pe.matmul(bank, xT[:, k, :], we[:, 512 * h:512 * h + 512], start=False, stop=True)
                        mm.then_inc(s_y, 1)

            @block.vector
            def _(dve):
                dve.sem_inc(s_used, 4)
                step = Chain(dve, s_dve)
                step(dve.tensor_reduce(top[:, :], logits[:, :, :], AXX, ALU.max))
                dve.tensor_tensor(ex[:, :, :], logits[:, :, :], spread(top[:, :], E, 2), ALU.subtract)\
                   .then_inc(s_shift, 1)
                dve.wait_ge(s_exp, 1)
                for n in range(2):
                    step(dve.tensor_reduce(top[:, :], ex[:, :, :], AXX, ALU.max))
                    step(dve.tensor_tensor(w[:, :, :], ex[:, :, :], spread(top[:, :], E, 2), ALU.is_equal))
                    step(dve.tensor_tensor(w[:, :, :], w[:, :, :], spread(C["rank"][:, :], nt, 1), ALU.mult))
                    step(dve.tensor_reduce(wm[:, :], w[:, :, :], AXX, ALU.max))
                    step(dve.tensor_tensor(hot[:, n, :, :], w[:, :, :], spread(wm[:, :], E, 2), ALU.is_equal))
                    step(dve.tensor_tensor(hot[:, n, :, :], hot[:, n, :, :], spread(top[:, :], E, 2), ALU.mult))
                    if n == 0:
                        step(dve.scalar_tensor_tensor(ex[:, :, :], hot[:, 0, :, :], -2.0, ex[:, :, :],
                                                      ALU.mult, ALU.add))
                step(dve.tensor_tensor(gates[:, :, :], hot[:, 0, :, :], hot[:, 1, :, :], ALU.add))
                step(dve.tensor_reduce(wm[:, :], gates[:, :, :], AXX, ALU.add))
                step(dve.reciprocal(top[:, :], wm[:, :]))
                step(dve.scalar_tensor_tensor(gates[:, :, :], gates[:, :, :], 0.5, spread(top[:, :], E, 2),
                                              ALU.mult, ALU.mult))
                with dve.Fori(0, nt // 4) as i:
                    for k in (0, 2):
                        for e in range(E):
                            for kk in (k, k + 1):
                                t = i * 4 + kk
                                if e == 0:
                                    dve.wait_ge(s_y, 4 + t + 1)
                                else:
                                    dve.wait_ge(s_acc, i * 4 * E + k * E + 2 * e - 1 + (kk - k))
                                xt = x[:, bass.ds(t, 1), :].rearrange("p a d -> p (a d)")
                                ins = dve.scalar_tensor_tensor(
                                    xt, ps[:, 2 * kk + e // 4, (e % 4) * D:(e % 4 + 1) * D],
                                    gates[:, bass.ds(t, 1), e:e + 1].rearrange("p a d -> p (a d)"), xt,
                                    ALU.mult, ALU.add).then_inc(s_acc, 1)
                        dve.wait_ge(s_acc, i * 4 * E + (k + 2) * E)
                        dve.sem_inc(s_used, 2)


def choose_tokens(nc, C, name, logits, cap, slot_id, slot_gate):
    nt, E = logits.shape[1], 8
    HI = cap // P
    F = 5
    with Stage(nc, name) as st:
        ps = st.banks()
        top = st.sb("top", [P, nt])
        ex = st.sb("exps", [P, nt, E])
        score = st.sb("score", [P, E, nt])
        thr, cand, add = (st.sb(n, [P, E], U32) for n in ("threshold", "candidate", "bit_kept"))
        hit = st.sb("hit", [P, E, nt], BF16)
        cnt = st.sb("count", [P, E], BF16)
        above, equal = st.sb("above", [P, E, nt], BF16), st.sb("equal", [P, E, nt], BF16)
        room = st.sb("room", [P, E])
        chosen = st.sb("chosen", [P, E, nt], BF16)
        scan = [st.sb(f"scan{k}", [P, E, nt]) for k in range(2)]
        pos = st.sb("position", [P, E, nt])
        pos_i, lo_i, hi_i = (st.sb(n, [P, E, nt], U32) for n in ("position_int", "lo_int", "hi_int"))
        lo, hi = st.sb("lo", [P, E, nt]), st.sb("hi", [P, E, nt])
        rest = st.sb("score_rest", [P, E, nt])
        part = st.sb("score_part", [P, 3, E, nt], BF16)
        pcol = st.sb("token_in_tile", [P, 1])
        tcol = st.sb("tile_number", [P, nt], BF16)
        hcol = st.sb("hi_number", [P, HI])
        lcol = st.sb("lo_number", [P, P], BF16)
        hot_hi = st.sb("hot_hi", [P, E * nt, HI], BF16)
        fields = st.sb("fields", [P, F, E * nt, HI], BF16)
        lo_bf = st.sb("lo_bf", [P, E, nt], BF16)
        hot_lo = st.sb("hot_lo", [P, 4, E, P], BF16)
        got = st.sb("got", [P, E, F, HI])
        s_exp, s_shift, s_dve, s_const = st.sem("exps"), st.sem("shifted"), st.sem("dve_chain"), st.sem("numbers")
        s_loop = st.sem("search_chain")
        s_cnt, s_sum = st.sem("count_ready"), st.sem("sum_ready")
        s_eq, s_pre, s_pre_used = st.sem("mask_ready"), st.sem("prefix_ready"), st.sem("room_ready")
        s_hot, s_lo = st.sem("hot_ready"), st.sem("lo_ready")
        s_fields, s_pick = st.sem("fields_ready"), st.sem("picked")
        p_sum = ps[:, 0, 0:E]
        p_pre = ps[:, 1, 0:E * nt]
        p_tot = ps[:, 2, 0:E * nt]
        p_got = ps[:, 3, 0:E * F * HI]
        p_sum2 = ps[:, 4, 0:E]

        with nc.Block() as block:

            @block.gpsimd
            def _(pool):
                kw = dict(channel_multiplier=0, base=0, allow_small_or_imprecise_dtypes=True)
                pool.iota(pcol[:, :], pattern=[[0, 1]], base=0, channel_multiplier=1,
                          allow_small_or_imprecise_dtypes=True).then_inc(s_const, 1)
                pool.iota(tcol[:, :], pattern=[[1, nt]], **kw).then_inc(s_const, 1)
                pool.iota(hcol[:, :], pattern=[[1, HI]], **kw).then_inc(s_const, 1)
                pool.iota(lcol[:, :], pattern=[[1, P]], **kw).then_inc(s_const, 1)

            @block.scalar
            def _(act):
                act.wait_ge(s_shift, 1)
                act.activation(ex[:, :, :], ex[:, :, :], ACT.Exp).then_inc(s_exp, 1)

            @block.tensor
            def _(pe):
                pe.sem_inc(s_pick, 4)
                with pe.Fori(0, BITS // 6) as i:
                    for k in range(6):
                        pe.wait_ge(s_cnt, i * 6 + k + 1)
                        pe.matmul(p_sum, C["ones_bf"][:, :], cnt[:, :], start=True, stop=True).then_inc(s_sum, 1)
                pe.wait_ge(s_cnt, BITS + 1)
                pe.matmul(p_sum2, C["ones_bf"][:, :], cnt[:, :], start=True, stop=True).then_inc(s_sum, 1)
                for n, mask in enumerate((equal, chosen)):
                    pe.wait_ge(s_eq, n + 1)
                    m = mask[:, :, :].rearrange("p e t -> p (e t)")
                    pe.matmul(p_pre, C["upto_bf"][:, :], m, start=True, stop=True)
                    pe.matmul(p_tot, C["ones_bf"][:, :], m, start=True, stop=True).then_inc(s_pre, 1)
                pe.wait_ge(s_fields, 1)
                with pe.Fori(0, nt // 4) as i:
                    for u in range(4):
                        pe.wait_ge(s_hot, i * 4 + u + 1)
                        for e in range(E):
                            mm = pe.matmul(
                                p_got[:, e * F * HI:(e + 1) * F * HI].rearrange("p (f h) -> p f h", f=F),
                                hot_lo[:, u, e, :],
                                fields[:, :, bass.ds(i * 4 + u + e * nt, 1), :].rearrange("p f a h -> p f (a h)"),
                                start=False, stop=False, skip_group_check=True)
                        mm.then_inc(s_pick, 1)

            @block.vector
            def _(dve):
                step = Chain(dve, s_dve)
                step(dve.tensor_reduce(top[:, :], logits[:, :, :], AXX, ALU.max))
                dve.tensor_tensor(ex[:, :, :], logits[:, :, :], spread(top[:, :], E, 2), ALU.subtract)\
                   .then_inc(s_shift, 1)
                dve.wait_ge(s_exp, 1)
                step(dve.tensor_reduce(top[:, :], ex[:, :, :], AXX, ALU.add))
                step(dve.reciprocal(top[:, :], top[:, :]))
                step(dve.tensor_tensor(score[:, :, :], ex[:, :, :].rearrange("p t e -> p e t"),
                                       spread(top[:, :], E, 1), ALU.mult))
                dve.memset(p_got, 0.0)
                step(dve.memset(thr[:, :], 0))
                LOOP, UN = 4, 6
                with dve.Fori(0, BITS // UN) as i:
                    for k in range(UN):
                        n = i * UN + k
                        go = Chain(dve, s_loop, n * LOOP)
                        bit, bit_i = (C[m][:, bass.ds(n, 1), :].rearrange("p a e -> p (a e)") for m in ("bit", "bit_i"))
                        go(dve.tensor_tensor(cand[:, :], thr[:, :], bit_i, ALU.bitwise_or))
                        go(dve.tensor_tensor(hit[:, :, :], score[:, :, :], spread(cand[:, :].bitcast(F32), nt, 2),
                                             ALU.is_ge))
                        with nc.allow_low_precision("counts up to the number of tiles"):
                            dve.tensor_reduce(cnt[:, :], hit[:, :, :], AXX, ALU.add).then_inc(s_cnt, 1)
                        dve.wait_ge(s_sum, n + 1)
                        go(dve.scalar_tensor_tensor(add[:, :], p_sum, float(cap), bit, ALU.is_ge, ALU.mult))
                        go(dve.tensor_tensor(thr[:, :], thr[:, :], add[:, :], ALU.bitwise_or))
                        assert go.n == LOOP
                T = spread(thr[:, :].bitcast(F32), nt, 2)
                step(dve.tensor_tensor(above[:, :, :], score[:, :, :], T, ALU.is_gt))
                dve.tensor_tensor(equal[:, :, :], score[:, :, :], T, ALU.is_equal).then_inc(s_eq, 1)
                with nc.allow_low_precision("counts up to the number of tiles"):
                    dve.tensor_reduce(cnt[:, :], above[:, :, :], AXX, ALU.add).then_inc(s_cnt, 1)
                dve.wait_ge(s_sum, BITS + 1)
                step(dve.tensor_scalar(room[:, :], p_sum2, -1.0, float(cap), ALU.mult, ALU.add))

                def ranks(n):
                    dve.wait_ge(s_pre, n + 1)
                    tot = p_tot.rearrange("p (e t) -> p e t", e=E)
                    step(dve.memset(scan[0][:, :, 0:1], 0.0))
                    step(dve.tensor_copy(scan[0][:, :, 1:nt], tot[:, :, 0:nt - 1]))
                    a, s = 0, 1
                    while s < nt:
                        step(dve.tensor_tensor(scan[1 - a][:, :, s:nt], scan[a][:, :, s:nt],
                                               scan[a][:, :, 0:nt - s], ALU.add))
                        step(dve.tensor_copy(scan[1 - a][:, :, 0:s], scan[a][:, :, 0:s]))
                        a, s = 1 - a, 2 * s
                    step(dve.tensor_tensor(pos[:, :, :], p_pre.rearrange("p (e t) -> p e t", e=E),
                                           scan[a][:, :, :], ALU.add))

                ranks(0)
                step(dve.tensor_tensor(pos[:, :, :], pos[:, :, :], spread(room[:, :], nt, 2), ALU.is_le))
                step(dve.tensor_tensor(equal[:, :, :], equal[:, :, :], pos[:, :, :], ALU.mult))
                dve.tensor_tensor(chosen[:, :, :], above[:, :, :], equal[:, :, :], ALU.add).then_inc(s_eq, 1)
                ranks(1)
                step(dve.tensor_scalar(pos[:, :, :], pos[:, :, :], -1.0, 0.0, ALU.add, ALU.max))
                step(dve.tensor_copy(pos_i[:, :, :], pos[:, :, :]))
                step(dve.tensor_scalar(lo_i[:, :, :], pos_i[:, :, :], P - 1, None, ALU.bitwise_and))
                step(dve.tensor_scalar(hi_i[:, :, :], pos_i[:, :, :], 7, None, ALU.logical_shift_right))
                step(dve.tensor_copy(lo[:, :, :], lo_i[:, :, :]))
                step(dve.tensor_copy(hi[:, :, :], hi_i[:, :, :]))
                step(dve.scalar_tensor_tensor(lo[:, :, :], lo[:, :, :], 1.0, chosen[:, :, :], ALU.add, ALU.mult))
                dve.tensor_scalar(lo_bf[:, :, :], lo[:, :, :], -1.0, None, ALU.add).then_inc(s_lo, 1)
                step(dve.tensor_copy(part[:, 0, :, :], score[:, :, :]))
                step(dve.tensor_tensor(rest[:, :, :], score[:, :, :], part[:, 0, :, :], ALU.subtract))
                step(dve.tensor_copy(part[:, 1, :, :], rest[:, :, :]))
                step(dve.tensor_tensor(part[:, 2, :, :], rest[:, :, :], part[:, 1, :, :], ALU.subtract))
                dve.wait_ge(s_const, 4)
                flat = "p e t -> p (e t)"
                step(dve.tensor_tensor(hot_hi[:, :, :], spread(hi[:, :, :].rearrange(flat), HI, 2),
                                       spread(hcol[:, :], E * nt, 1), ALU.is_equal))
                step(dve.tensor_scalar(fields[:, 0, :, :], hot_hi[:, :, :], pcol[:, 0:1], None, ALU.mult))
                for e in range(E):
                    step(dve.tensor_tensor(fields[:, 1, e * nt:(e + 1) * nt, :], hot_hi[:, e * nt:(e + 1) * nt, :],
                                           spread(tcol[:, :], HI, 2), ALU.mult))
                for k in range(3):
                    step(dve.tensor_tensor(fields[:, 2 + k, :, :], hot_hi[:, :, :],
                                           spread(part[:, k, :, :].rearrange(flat), HI, 2), ALU.mult))
                dve.sem_inc(s_fields, 1)
                dve.wait_ge(s_lo, 1)
                with dve.Fori(0, nt // 4) as i:
                    for u in range(4):
                        dve.wait_ge(s_pick, i * 4 + u + 1)
                        dve.tensor_tensor(hot_lo[:, u, :, :], spread(lcol[:, :], E, 1),
                                          lo_bf[:, :, bass.ds(i * 4 + u, 1)].broadcast_to([P, E, P]),
                                          ALU.is_equal).then_inc(s_hot, 1)
                dve.wait_ge(s_pick, 4 + nt)
                step(dve.tensor_copy(got[:, :, :, :], p_got.rearrange("p (e f h) -> p e f h", e=E, f=F)))
                step(dve.scalar_tensor_tensor(slot_id[:, :, :], got[:, :, 1, :], float(P), got[:, :, 0, :],
                                              ALU.mult, ALU.add))
                step(dve.tensor_tensor(got[:, :, 2, :], got[:, :, 2, :], got[:, :, 3, :], ALU.add))
                step(dve.tensor_tensor(got[:, :, 2, :], got[:, :, 2, :], got[:, :, 4, :], ALU.add))
                step(dve.tensor_scalar(slot_gate[:, :, :], got[:, :, 2, :], 0.5, None, ALU.mult))


def expert_mlps(nc, C, name, x, xn_rows, acc_rows, slot_id, slot_gate, W1, b1col, W2, bias_at):
    E, HI = slot_id.shape[1], slot_id.shape[2]
    NH = W1.shape[2] // P
    with Stage(nc, name) as st:
        ps = st.banks()
        w1 = st.sb("w1", [P, 2, NH * P])
        w2 = st.sb("w2", [P, 2, NH, D])
        ids_in = st.sb("ids_gathered", [P, 2, HI], U32)
        ids_out = st.sb("ids_added", [P, 2, HI], U32)
        b1 = st.sb("b1", [P, 2, NH])
        gate = st.sb("gate", [P, 2, HI])
        xg = st.sb("xg", [P, 2, HI, D])
        xgT = st.sb("xgT", [P, 2, SEQ])
        b2r = st.sb("b2", [3, 2, D], BF16)
        h = st.sb("hidden", [P, 2, NH, SEQ])
        y = st.sb("y", [P, 2, HI, D])
        s_w = st.sem("weights_ready")
        s_w1, s_w2 = st.sem("w1_landed"), st.sem("w2_landed")
        s_ids, s_small = st.sem("ids_ready"), st.sem("gate_and_biases_ready")
        s_g = [[st.sem(f"gathered_{k}{g}") for g in range(2)] for k in "ab"]
        s_sc = st.sem("scattered")
        s_tp, s_tev = st.sem("transposed"), st.sem("xgT_ready")
        s_h, s_gelu = st.sem("hidden_ready"), st.sem("gelu_ready")
        s_y, s_yev = st.sem("y_ready"), st.sem("y_scaled")
        s_added, s_seen = st.sem("experts_added"), st.sem("pool_has_seen")
        s_back = st.sem("x_back")
        with nc.Block() as block:

            @block.sync
            def _(sp):
                with sp.Fori(0, E // 2) as i:
                    for u in range(2):
                        e = i * 2 + u
                        sp.wait_ge(s_y, 1 + i * 4)
                        sp.dma_start(w1[:, u, :], W1[bass.ds(e, 1), :, :].rearrange("a d f -> d (a f)"))\
                          .then_inc(s_w1, 16)
                        sp.dma_start(w2[:, u, :, :], W2[bass.ds(e, 1), :, :].rearrange("a (c f) d -> f (a c) d", f=P))\
                          .then_inc(s_w2, 16)
                        sp.wait_ge(s_w1, e * 16 + 16)
                        sp.wait_ge(s_w2, e * 16 + 16)
                        sp.sem_inc(s_w, 1)
                sp.wait_ge(s_sc, E * HI * 16)
                sp.dma_start(x[:, :, :], acc_rows.rearrange("(t p) d -> p t d", p=P)).then_inc(s_back, 16)
                sp.wait_ge(s_back, 16)

            @block.gpsimd
            def _(pool):
                pool.sem_inc(s_added, 2)

                def gather(e, u):
                    pool.tensor_copy(ids_in[:, u, :], slot_id[:, bass.ds(e, 1), :].rearrange("p a h -> p (a h)"))\
                        .then_inc(s_ids, 1)
                    pool.wait_ge(s_ids, e + 1)
                    pool.sem_inc(s_seen, 1)
                    for k in range(HI):
                        pool.indirect_dma_start(
                            xg[:, u, k, :], None, xn_rows,
                            bass.IndirectOffsetOnAxis(ap=ids_in[:, u, k:k + 1], axis=0)).then_inc(s_g[u][k // 4], 16)

                def fetch_small(e, u):
                    for dst, src in (
                            (ids_out[:, u, :], slot_id[:, bass.ds(e, 1), :].rearrange("p a h -> p (a h)")),
                            (gate[:, u, :], slot_gate[:, bass.ds(e, 1), :].rearrange("p a h -> p (a h)")),
                            (b1[:, u, :], b1col[:, bass.ds(e, 1), :].rearrange("p a h -> p (a h)")),
                            (b2r[:, u, :], C["bias_rows"][:, bass.ds(e * D + bias_at, D)])):
                        pool.tensor_copy(dst, src).then_inc(s_small, 1)

                def add(e, u):
                    for k in range(HI):
                        if k % 4 == 0:
                            pool.wait_ge(s_yev, 1 + e * 2 + k // 4 + 1)
                            pool.sem_inc(s_seen, 1)
                            pool.wait_ge(s_small, e * 4 + 4)
                            pool.sem_inc(s_seen, 1)
                        pool.indirect_dma_start(
                            acc_rows, bass.IndirectOffsetOnAxis(ap=ids_out[:, u, k:k + 1], axis=0),
                            y[:, u, k, :], None, compute_op=ALU.add).then_inc(s_sc, 16)
                    pool.wait_ge(s_sc, e * HI * 16 + HI * 16)
                    pool.sem_inc(s_added, 1)

                for u in range(2):
                    gather(u, u)
                    fetch_small(u, u)
                with pool.Fori(0, E // 2 - 1) as i:
                    for u in range(2):
                        e = i * 2 + u
                        pool.wait_ge(s_tp, 1 + e * 2 + 2)
                        pool.sem_inc(s_seen, 1)
                        gather(e + 2, u)
                        add(e, u)
                        fetch_small(e + 2, u)
                for u in range(2):
                    add(E - 2 + u, u)

            @block.tensor
            def _(pe):
                pe.sem_inc(s_y, 1)
                pe.sem_inc(s_tp, 1)
                pe.sem_inc(s_h, 1)
                pT, pY = [ps[:, 0, :], ps[:, 1, :]], [ps[:, 2, :], ps[:, 3, :]]

                def transposes(i, m):
                    u, g = m // 2, m % 2
                    n = i * 4 + m
                    pe.wait_ge(s_g[u][g], i * HI * 8 + HI * 8)
                    pe.wait_ge(s_tev, 1 + i * 4 + max(m - 1, 0))
                    for k in range(4):
                        mm = pe.transpose(pT[m % 2][:, k * P:(k + 1) * P], xg[:, u, 4 * g + k, :], C["ident"][:, :])
                    mm.then_inc(s_tp, 1)

                def first(i, m):
                    u = m // 2
                    pe.wait_ge(s_w, i * 2 + u + 1)
                    pe.wait_ge(s_tev, 1 + i * 4 + m + 1)
                    for c in range(NH):
                        pe.wait_ge(s_gelu, 1 + i * 16 + m * 4 + c - 3 if m or c == 3 else i * 16)
                        pe.matmul(ps[:, 4 + c, :], w1[:, u, c * P:(c + 1) * P], xgT[:, m % 2, :],
                                  start=True, stop=True).then_inc(s_h, 1)

                def second(i, m):
                    u = m // 2
                    pe.wait_ge(s_gelu, 1 + i * 16 + m * 4 + 4)
                    pe.wait_ge(s_small, (i * 2 + u) * 4 + 4)
                    pe.wait_ge(s_yev, 1 + i * 4 + max(m - 1, 0))
                    for k in range(4):
                        o = pY[m % 2][:, k * D:(k + 1) * D]
                        pe.matmul(o, C["ones_bf"][0:3, :], b2r[:, u, :], start=(k == 0), stop=False,
                                  skip_group_check=True)
                        for c in range(NH):
                            mm = pe.matmul(o, h[:, m % 2, c, k * P:(k + 1) * P], w2[:, u, c, :], start=False,
                                           stop=False, skip_group_check=True)
                    mm.then_inc(s_y, 1)

                with pe.Fori(0, E // 2) as i:
                    transposes(i, 0)
                    for m in range(4):
                        first(i, m)
                        if m < 3:
                            transposes(i, m + 1)
                        if m > 0:
                            second(i, m - 1)
                    second(i, 3)

            @block.scalar
            def _(act):
                act.sem_inc(s_gelu, 1)
                with act.Fori(0, E // 2) as i:
                    for m in range(4):
                        u = m // 2
                        act.wait_ge(s_small, (i * 2 + u) * 4 + 4)
                        for c in range(NH):
                            act.wait_ge(s_h, 1 + i * 16 + m * 4 + c + 1)
                            act.wait_ge(s_y, 1 + i * 4 + max(m - 1, 0))
                            act.activation(h[:, m % 2, c, :], ps[:, 4 + c, :], ACT.Gelu, bias=b1[:, u, c:c + 1])\
                               .then_inc(s_gelu, 1)

            @block.vector
            def _(dve):
                dve.sem_inc(s_tev, 1)
                dve.sem_inc(s_yev, 1)
                def evac(i, m):
                    dve.wait_ge(s_tp, 1 + i * 4 + m + 1)
                    dve.wait_ge(s_h, 1 + i * 16 + 4 * max(m - 1, 0))
                    dve.tensor_copy(xgT[:, m % 2, :], ps[:, m % 2, :]).then_inc(s_tev, 1)

                with dve.Fori(0, E // 2) as i:
                    evac(i, 0)
                    for m in range(4):
                        u, g = m // 2, m % 2
                        if m < 3:
                            evac(i, m + 1)
                        dve.wait_ge(s_small, (i * 2 + u) * 4 + 4)
                        dve.wait_ge(s_y, 1 + i * 4 + m + 1)
                        dve.wait_ge(s_added, i * 2 + u + 1)
                        dve.tensor_tensor(y[:, u, 4 * g:4 * g + 4, :],
                                          ps[:, 2 + m % 2, :].rearrange("p (k d) -> p k d", k=4),
                                          spread(gate[:, u, 4 * g:4 * g + 4], D, 2), ALU.mult).then_inc(s_yev, 1)


NH, HD = 16, 8
VC = HD + 1
ROWS = 48
Q_PARTS = (0, 0, 0, 1, 1, 2)
K_PARTS = (0, 1, 2, 0, 1, 0)


def project(nc, C, name, xT_all, Wq, Wk, Wv, q_stack, k_stack, v_all, bq=None, bk=None, v_bias=None,
            linear=None):
    nb = xT_all.shape[1] // SEQ
    with Stage(nc, name) as st:
        ps = st.banks()
        xc = st.sb("x_chunk", [P, 2, SEQ])
        f = st.sb("qk", [P, 2, 2, SEQ])
        rest = st.sb("rest", [P, 2, 2, SEQ])
        parts = st.sb("parts", [P, 2, 2, 3, SEQ], BF16)
        e1 = st.sb("exps", [P, 3, SEQ])
        r1 = st.sb("relus", [P, 3, SEQ])
        s_x, s_qk, s_v, s_vev = st.sem("x_ready"), st.sem("qk_ready"), st.sem("v_ready"), st.sem("v_kept")
        s_f, s_hi, s_rest, s_mid, s_low = (st.sem(n) for n in ("qk_final", "high_ready", "rest_ready",
                                                               "middle_ready", "low_ready"))
        s_out = [st.sem(f"stacks_stored_{k}") for k in "ab"]
        s_ones, s_e, s_t = st.sem("ones_set"), st.sem("exp_ready"), st.sem("dve_chain")
        s_kt_ev, s_q_ev, s_seen = st.sem("k_token_kept"), st.sem("q_kept"), st.sem("pool_has_seen")
        with nc.Block() as block:

            @block.gpsimd
            def _(pool):
                pool.memset(v_all[:, :, :, HD:VC], 1.0).then_inc(s_ones, 1)
                if linear:
                    pool.sem_inc(s_q_ev, 2)
                with pool.Fori(0, nb // 2) as i:
                    for u in range(2):
                        c = i * 2 + u
                        pool.wait_ge(s_v, c + 1)
                        pool.sem_inc(s_seen, 1)
                        pool.tensor_copy(xc[:, u, :], xT_all[:, bass.ds(c * SEQ, SEQ)]).then_inc(s_x, 1)
                    if linear:
                        for u in range(2):
                            c = i * 2 + u
                            pool.wait_ge(s_f, 4 + c * 2 + 1)
                            pool.sem_inc(s_seen, 1)
                            pool.tensor_copy(linear["q"][:, bass.ds(c * SEQ, SEQ)], f[:, u, 0, :]).then_inc(s_q_ev, 1)

            @block.tensor
            def _(pe):
                pe.sem_inc(s_v, 2)
                with pe.Fori(0, nb // 2) as i:
                    for u in range(2):
                        c = i * 2 + u
                        pe.wait_ge(s_x, c + 1)
                        pe.wait_ge(s_f, c * 2 + 2)
                        pe.matmul(ps[:, u, :], Wq, xc[:, u, :], start=True, stop=True).then_inc(s_qk, 1)
                        pe.matmul(ps[:, 2 + u, :], Wk, xc[:, u, :], start=True, stop=True).then_inc(s_qk, 1)
                        pe.wait_ge(s_vev, c + 1)
                        for k in range(4):
                            o = ps[:, 4 + u, k * P:(k + 1) * P]
                            if v_bias is not None:
                                pe.matmul(o, C["ones_bf"][0:3, :], C["bias_rows"][:, v_bias:v_bias + P],
                                          start=(k == 0), stop=False, skip_group_check=True)
                            mm = pe.matmul(o, xc[:, u, k * P:(k + 1) * P], Wv, start=(k == 0 and v_bias is None),
                                           stop=False, skip_group_check=True)
                        if linear:
                            pe.wait_ge(s_kt_ev, c + 1)
                            for k in range(4):
                                o = ps[:, 6 + u, k * P:(k + 1) * P]
                                pe.matmul(o, C["ones_bf"][0:3, :],
                                          C["bias_rows"][:, linear["k_bias"]:linear["k_bias"] + P],
                                          start=(k == 0), stop=False, skip_group_check=True)
                                mm = pe.matmul(o, xc[:, u, k * P:(k + 1) * P], Wk, start=False, stop=False,
                                               skip_group_check=True)
                        mm.then_inc(s_v, 1)

            @block.scalar
            def _(act):
                if not linear:
                    act.sem_inc(s_f, 4)
                act.sem_inc(s_hi, 4)
                act.sem_inc(s_mid, 4)
                with act.Fori(0, nb // 2) as i:
                    for u in range(2):
                        c = i * 2 + u
                        if linear:
                            for n in range(3):
                                if n < 2:
                                    act.wait_ge(s_qk, c * 2 + n + 1)
                                    kw = dict(bias=(bq, bk)[n], scale=(linear["scale"], 1.0)[n])
                                else:
                                    act.wait_ge(s_v, 2 + c + 1)
                                    kw = {}
                                act.wait_ge(s_t, c * 6 + 2 * n + 2)
                                src = ps[:, 2 * n + u, :] if n < 2 else ps[:, 6 + u, :]
                                act.activation(e1[:, n, :], src, ACT.Exp, **kw).then_inc(s_e, 1)
                                act.activation(r1[:, n, :], src, ACT.Relu, **kw).then_inc(s_e, 1)
                        else:
                            for n in range(2):
                                act.wait_ge(s_qk, c * 2 + n + 1)
                                act.wait_ge(s_rest, c * 2 + n + 1)
                                kw = dict(bias=(bq, bk)[n]) if bq is not None else {}
                                act.activation(f[:, u, n, :], ps[:, 2 * n + u, :],
                                               ACT.Identity if kw else ACT.Copy, **kw).then_inc(s_f, 1)
                        for n in range(2):
                            act.wait_ge(s_f, 4 + c * 2 + n + 1)
                            act.wait_ge(s_out[u], 1 + i * 96)
                            act.activation(parts[:, u, n, 0, :], f[:, u, n, :], ACT.Copy).then_inc(s_hi, 1)
                        for n in range(2):
                            act.wait_ge(s_rest, 4 + c * 2 + n + 1)
                            act.activation(parts[:, u, n, 1, :], rest[:, u, n, :], ACT.Copy).then_inc(s_mid, 1)

            @block.vector
            def _(dve):
                if linear:
                    dve.sem_inc(s_f, 4)
                    dve.sem_inc(s_kt_ev, 2)
                    dve.sem_inc(s_t, 6)
                dve.sem_inc(s_vev, 2)
                dve.sem_inc(s_rest, 4)
                with dve.Fori(0, nb // 2) as i:
                    for u in range(2):
                        c = i * 2 + u
                        if linear:
                            step = Chain(dve, s_t, 6 + c * 6)
                            for n in range(3):
                                dve.wait_ge(s_e, c * 6 + 2 * n + 2)
                                step(dve.tensor_scalar(e1[:, n, :], e1[:, n, :], 1.0, 0.0001, ALU.min, ALU.add))
                                if n < 2:
                                    dve.wait_ge(s_hi, c * 2 + n + 1)
                                    if n == 0:
                                        dve.wait_ge(s_q_ev, c + 1)
                                    out = f[:, u, n, :]
                                else:
                                    out = linear["k"][:, bass.ds(c * SEQ, SEQ)]
                                step(dve.tensor_tensor(out, e1[:, n, :], r1[:, n, :], ALU.add))
                                dve.sem_inc(s_f if n < 2 else s_kt_ev, 1)
                        dve.wait_ge(s_v, 2 + c + 1)
                        dve.tensor_copy(v_all[:, bass.ds(c * 4, 4), :, 0:HD],
                                        ps[:, 4 + u, :].rearrange("p (t h e) -> p t h e", t=4, h=NH))\
                           .then_inc(s_vev, 1)
                        for n in range(2):
                            dve.wait_ge(s_hi, 4 + c * 2 + n + 1)
                            dve.wait_ge(s_mid, c * 2 + n + 1)
                            dve.tensor_tensor(rest[:, u, n, :], f[:, u, n, :], parts[:, u, n, 0, :], ALU.subtract)\
                               .then_inc(s_rest, 1)
                        for n in range(2):
                            dve.wait_ge(s_mid, 4 + c * 2 + n + 1)
                            dve.tensor_tensor(parts[:, u, n, 2, :], rest[:, u, n, :], parts[:, u, n, 1, :],
                                              ALU.subtract).then_inc(s_low, 1)

            @block.sync
            def _(sp):
                for u in range(2):
                    sp.sem_inc(s_out[u], 1)
                with sp.Fori(0, nb // 2) as i:
                    for u in range(2):
                        c = i * 2 + u
                        for n, (stack, which) in enumerate(((q_stack, Q_PARTS), (k_stack, K_PARTS))):
                            sp.wait_ge(s_low, c * 2 + n + 1)
                            rows = stack[bass.ds(c, 1), :, :, :].rearrange("a h (e k) n -> (a h e) k n", k=6)
                            for first, copies in ((0, 3), (3, 2), (5, 1)):
                                part = which[first]
                                if n == 0:
                                    src = spread(parts[:, u, n, part, :], copies, 1)
                                else:
                                    src = parts[:, u, n, 0:copies, :]
                                sp.dma_start(rows[:, first:first + copies, :], src).then_inc(s_out[u], 16)
                for u in range(2):
                    sp.wait_ge(s_out[u], 1 + 96 * (nb // 2))


def window_attention(nc, C, name, q_stack, k_stack, v_all, causal, x=None, Wo=None, oT_all=None):
    nb = q_stack.shape[0]
    SCALE = HD ** -0.5
    per1 = 2 if causal else 1
    per2 = 4 if causal else 2
    W = 256 if causal else 512
    U1, U2 = 16 // per1, 16 // per2
    R = U1 // U2
    MAX_ROW = 64 + ROWS
    RU = U2 // 4
    NB = 8
    AHEAD = NB // RU
    LAG = 3 if RU == 2 else 2
    AT_MAX, AT_SUMS = 1, (3 if RU == 2 else 2)
    AT_SEQ, AT_OUT = (5, 7) if RU == 2 else (3, 3)
    if causal:
        keys = [[(k, {-1: "col_gt", 0: "col_le"}[k - i]) for k in range(max(i - 1, 0), i + 1)] for i in range(4)]
        queries = [[(i, {0: "col_ge", 1: "col_lt"}[i - k]) for i in range(k, min(k + 1, 3) + 1)] for k in range(4)]
    else:
        keys = [[(k, {-1: "col_ge", 0: None, 1: "col_le"}[k - i]) for k in range(max(i - 1, 0), min(i + 1, 3) + 1)]
                for i in range(4)]
        queries = [[(i, {-1: "col_ge", 0: None, 1: "col_le"}[i - k])
                    for i in range(max(k - 1, 0), min(k + 1, 3) + 1)] for k in range(4)]
    if causal:
        units1 = [(i, [(hh, 0), (hh, 1)]) for i in range(4) for hh in range(2)]
        units2 = [(k, [(0, 0), (0, 1), (1, 0), (1, 1)]) for k in range(4)]
    else:
        units1 = [(i, [(hh, pr)]) for i in range(4) for pr in range(2) for hh in range(2)]
        units2 = [(k, [(0, pr), (1, pr)]) for k in range(4) for pr in range(2)]
    with Stage(nc, name) as st:
        ps = st.banks()
        qs = st.sb("q_rows", [P, 4, 1, 2, SEQ], BF16)
        ks = st.sb("k_rows", [P, 4, 2, 2, SEQ], BF16)
        ones = st.sb("ones", [3, 2 * SEQ], BF16)
        nmax = st.sb("minus_max", [P, 2, 4, 4])
        nrest = st.sb("minus_max_rest", [P, 2, 4, 4])
        nparts = st.sb("minus_max_parts", [P, 2, 4, 4, 3], BF16)
        nrow = st.sb("max_rows", [12, 2, SEQ], BF16)
        pt = st.sb("weights", [P, NB, 1024])
        rden = st.sb("one_over_sum", [P, 4, 4])
        vs = st.sb("values", [P, 4, 4, 4, 32])
        sT = st.sb("sums_T", [P, SEQ])
        oa = st.sb("attended", [P, 4, 2, 8 * HD])
        oT = st.sb("attended_T", [P, SEQ])
        s_load = [st.sem(f"group{g}_landed") for g in range(4)]
        s_ones, s_one_rows = st.sem("ones_set"), st.sem("one_rows_landed")
        s_p1, s_max, s_split = st.sem("scores1_ready"), st.sem("max_ready"), st.sem("max_split")
        s_chain, s_nt, s_nrow, s_mrow = st.sem("dve_chain"), st.sem("max_turned"), st.sem("max_rows_ready"), \
            st.sem("max_rows_landed")
        s_p2, s_exp, s_pv = st.sem("scores2_ready"), st.sem("weights_ready"), st.sem("weights_used")
        s_sel = st.sem("weights_masked")
        s_v, s_vz, s_seen = st.sem("values_ready"), st.sem("values_zeroed"), st.sem("pool_has_seen")
        s_sT, s_turn = st.sem("sums_T_ready"), st.sem("sums_turned")
        s_oev, s_rd = st.sem("sums_used"), st.sem("reciprocal")
        s_oT, s_oTc, s_y, s_yev = st.sem("attended_turned"), st.sem("attended_T_ready"), st.sem("out_ready"), \
            st.sem("out_added")
        turn = ps[:, 7, :]
        turn_bf = ps[0:12, 7, 0:256].bitcast(BF16)
        p_oT = ps[:, 6, :]
        p_o = turn.rearrange("p (i h c) -> p i h c", i=4, h=4)
        CH = 4

        def head(g, hh, prl):
            return 8 * hh + 2 * g + prl

        with nc.Block() as block:

            @block.sync
            def _(sp):
                sp.sem_inc(s_mrow, 1)
                def load(b, g):
                    for stack, dst in ((q_stack, qs), (k_stack, ks)):
                        for hh in range(2):
                            src = stack[bass.ds(b, 1), 8 * hh + 2 * g:8 * hh + 2 * g + 2, :, :]
                            sp.dma_start(dst[64 * hh:64 * hh + ROWS, g, hh if dst is ks else 0, :, :],
                                         src.rearrange("a h r n -> r (a h) n")).then_inc(s_load[g], 16)

                def max_rows(q, g, first=False):
                    sp.wait_ge(s_nrow, q + 1)
                    for hl in range(4):
                        hh, prl = hl // 2, hl % 2
                        sp.dma_start(qs[MAX_ROW + 3 * hh:MAX_ROW + 3 * hh + 3, g, 0, prl, :],
                                     nrow[3 * hl:3 * hl + 3, g % 2, :]).then_inc(s_mrow, 16)
                    sp.wait_ge(s_mrow, 1 + q * 64 + 64)

                def body(b, last):
                    for g in range(4):
                        q = b * 4 + g
                        if not (last and g == 3):
                            max_rows(q + 1, (g + 1) % 4)
                        if not last:
                            sp.wait_ge(s_p2, q * U2 + U2)
                            load(b + 1, g)

                sp.wait_ge(s_ones, 4)
                for g in range(4):
                    load(0, g)
                for hh in range(2):
                    sp.dma_start(ks[MAX_ROW + 3 * hh:MAX_ROW + 3 * hh + 3, :, hh, :, :]
                                 .rearrange("r g p n -> r g (p n)"), spread(ones[:, :], 4, 1))\
                        .then_inc(s_one_rows, 16)
                max_rows(0, 0)
                with sp.Fori(0, nb - 1) as b:
                    body(b, False)
                body(nb - 1, True)

            @block.gpsimd
            def _(pool):
                pool.memset(ones[:, :], 1.0).then_inc(s_ones, 1)
                pool.memset(ks[:, 0:2, :, :, :], 0.0).then_inc(s_ones, 1)
                pool.memset(vs[:, :, :, :, :], 0.0).then_inc(s_vz, 1)

                def copy_values(b, g):
                    for hh in range(2):
                        pool.tensor_copy(vs[:, g, :, 2 * hh:2 * hh + 2, 0:VC],
                                         v_all[:, bass.ds(b * 4, 4), 8 * hh + 2 * g:8 * hh + 2 * g + 2, :])\
                            .then_inc(s_v, 1)

                kept = {"col_ge": (0, 1, -1), "col_lt": (-1, -1, 1), "col_le": (0, -1, 1)}

                def group(b, g):
                    q = b * 4 + g
                    if not (isinstance(b, int) and b == nb - 1 and g >= 2):
                        if not isinstance(q, int) or q >= 2:
                            pool.wait_ge(s_pv, AHEAD + (q - 1) * 4)
                            pool.sem_inc(s_seen, 1)
                        copy_values(b + (1 if g >= 2 else 0), (g + 2) % 4)
                    for n in range(U2):
                        k, heads = units2[n]
                        pool.wait_ge(s_exp, 1 + q * U2 + n + 1)
                        pool.sem_inc(s_seen, 1)
                        w = len(queries[k]) * P
                        for i, mask in queries[k]:
                            if mask:
                                base, over_q, over_k = kept[mask]
                                at = (i - queries[k][0][0]) * P
                                o = pt[:, (g * U2 + n) % NB, 0:per2 * w].rearrange("p (h w) -> p h w", w=w)\
                                    [:, :, at:at + P]
                                ins = pool.affine_select(out=o, in_=o, compare_op=ALU.is_ge, fill=0.0, base=base,
                                                         pattern=[[0, per2], [over_q, P]],
                                                         channel_multiplier=over_k)
                        ins.then_inc(s_sel, 1)

                pool.wait_ge(s_vz, 1)
                for g in range(2):
                    copy_values(0, g)
                group(0, 0)
                with pool.Fori(0, nb - 1) as b:
                    for g in (1, 2, 3):
                        group(b, g)
                    group(b + 1, 0)
                for g in (1, 2, 3):
                    group(nb - 1, g)

            @block.tensor
            def _(pe):
                pe.sem_inc(s_pv, AHEAD)
                pe.sem_inc(s_oT, 1)
                pe.sem_inc(s_turn, 1)

                def pass1(b, q, g, n):
                    i, heads = units1[n]
                    if n == 0:
                        pe.wait_ge(s_load[g], b * 64 + 64)
                    u = q * U1 + n - 1
                    if not (isinstance(q, int) and u < 0):
                        pe.wait_ge(s_max, u)
                    bank = ps[:, n % 2, :]
                    k0, k1 = keys[i][0][0], keys[i][-1][0] + 1
                    for m, (hh, prl) in enumerate(heads):
                        pe.matmul(bank[:, m * W:m * W + (k1 - k0) * P], qs[0:MAX_ROW, g, 0, prl, i * P:(i + 1) * P],
                                  ks[0:MAX_ROW, g, hh, prl, k0 * P:k1 * P], start=(m == 0), stop=False,
                                  skip_group_check=True)
                    masked = [(k, mask) for k, mask in keys[i] if mask]
                    for k, mask in masked:
                        o = bank.rearrange("p (m w) -> p m w", w=W)[:, :, (k - k0) * P:(k - k0 + 1) * P]
                        mm = pe.matmul(o, C["ident_bf"][:, :], C[mask][:, 0:per1, :], start=False, stop=False,
                                       skip_group_check=True)
                    mm.then_inc(s_p1, 1)

                def pass2(q, g, n):
                    k, heads = units2[n]
                    if n == 0:
                        pe.wait_ge(s_mrow, 1 + q * 64 + 64)
                        if isinstance(q, int) and q == 0:
                            pe.wait_ge(s_one_rows, 32)
                    pe.wait_ge(s_exp, 1 + q * U2 + n - 1)
                    pair = ps[:, 2 + 2 * (n % 2):4 + 2 * (n % 2), :]
                    i0, i1 = queries[k][0][0], queries[k][-1][0] + 1
                    for hh, prl in heads:
                        at = prl * W if causal else 0
                        mm = pe.matmul(pair[:, hh, at:at + (i1 - i0) * P], ks[0:MAX_ROW + 6, g, hh, prl, k * P:(k + 1) * P],
                                       qs[0:MAX_ROW + 6, g, 0, prl, i0 * P:i1 * P], start=(at == 0), stop=False,
                                       skip_group_check=True)
                    mm.then_inc(s_p2, 1)

                def values(q, g, k):
                    pe.wait_ge(s_sel, q * U2 + (k + 1) * RU)
                    if k == 0:
                        pe.wait_ge(s_v, q * 2 + 2)
                        pe.wait_ge(s_sT, 1 + q)
                    i0 = queries[k][0][0]
                    w = len(queries[k]) * P
                    for hl in range(4):
                        hh, prl = hl // 2, hl % 2
                        n, m = (k, hl) if causal else (2 * k + prl, hh)
                        mm = pe.matmul(p_oT[32 * hl:32 * hl + 32, i0 * P:i0 * P + w], vs[:, g, k, hl, :],
                                       pt[:, (g * U2 + n) % NB, m * w:(m + 1) * w], start=(k == 0), stop=False,
                                       skip_group_check=True)
                    mm.then_inc(s_pv, 1)

                def turn_max(q, g, after=None):
                    pe.wait_ge(s_split, q + 1)
                    for i in range(4):
                        mm = pe.transpose(turn_bf[:, i * P:(i + 1) * P],
                                          nparts[:, g % 2, i, :, :].rearrange("p h c -> p (h c)"), C["ident_bf"][:, :])
                    mm.then_inc(s_nt, 1)

                def turn_sums(q):
                    pe.wait_ge(s_sT, 1 + q + 1)
                    for i in range(4):
                        mm = pe.transpose(turn[:, i * P:(i + 1) * P], sT[:, i * P:(i + 1) * P], C["ident"][:, :])
                    mm.then_inc(s_turn, 1)

                def turn_sequence(b):
                    pe.wait_ge(s_oev, 1 + b * 4 + 4)
                    for i in range(4):
                        mm = pe.transpose(turn[:, i * P:(i + 1) * P], oa[:, i, :, :].rearrange("p a c -> p (a c)"),
                                          C["ident"][:, :])
                    mm.then_inc(s_oT, 1)

                def project_out(b):
                    pe.wait_ge(s_oTc, 1 + b + 1)
                    for i in range(4):
                        mm = pe.matmul(turn[:, i * P:(i + 1) * P], oT[:, i * P:(i + 1) * P], Wo,
                                       start=(i == 0), stop=False, skip_group_check=True)
                    mm.then_inc(s_y, 1)

                def group(b, g, first=False, last=False):
                    q = b * 4 + g
                    for n in range(U2):
                        pass2(q, g, n)
                        if not (last and g >= 2):
                            for r in range(R):
                                pass1(b + (1 if g >= 2 else 0), q + 2, (g + 2) % 4, n * R + r)
                        if (n - LAG + 1) % RU == 0:
                            k = (n - LAG + 1) // RU - 1
                            if k >= 0:
                                values(q, g, k)
                            elif not first:
                                values(q - 1, (g - 1) % 4, k + 4)
                        if n == AT_MAX and not (last and g == 3):
                            pe.wait_ge(s_nrow, q + 1)
                            if not first:
                                pe.wait_ge(s_oev, q)
                            if g == 1 and not (isinstance(b, int) and b == 0):
                                pe.wait_ge(s_oTc, 1 + b)
                                if Wo is not None:
                                    pe.wait_ge(s_yev, 1 + b)
                            turn_max(q + 1, (g + 1) % 4)
                        if n == AT_SUMS and not first:
                            pe.wait_ge(s_nrow, q + (1 if last and g == 3 else 2))
                            pe.wait_ge(s_oev, q)
                            turn_sums(q - 1)
                        if n == AT_SEQ and g == 0 and not first:
                            turn_sequence(b - 1)
                        if n == AT_OUT and g == 0 and not first and Wo is not None:
                            project_out(b - 1)

                for g in range(2):
                    for n in range(U1):
                        pass1(0, g, g, n)
                turn_max(0, 0)
                group(0, 0, first=True)
                with pe.Fori(0, nb - 1) as b:
                    for g in (1, 2, 3):
                        group(b, g)
                    group(b + 1, 0)
                for g in (1, 2, 3):
                    group(nb - 1, g, last=True)
                for k in range((U2 - LAG) // RU, 4):
                    values(nb * 4 - 1, 3, k)
                pe.wait_ge(s_oev, nb * 4)
                turn_sums(nb * 4 - 1)
                turn_sequence(nb - 1)
                if Wo is not None:
                    project_out(nb - 1)

            @block.scalar
            def _(act):
                act.sem_inc(s_exp, 1)
                act.sem_inc(s_oTc, 1)
                act.sem_inc(s_sT, 1)
                def rows(q, g):
                    act.wait_ge(s_nt, q + 1)
                    if not isinstance(q, int) or q >= 1:
                        act.wait_ge(s_mrow, 1 + (q - 1) * 64)
                    act.activation(nrow[:, g % 2, :], turn_bf, ACT.Copy).then_inc(s_nrow, 1)

                def sums_T(q):
                    act.wait_ge(s_pv, AHEAD + q * 4 + 4)
                    act.wait_ge(s_turn, 1 + q)
                    act.activation(sT[:, :], p_oT, ACT.Copy).then_inc(s_sT, 1)

                def sequence_T(b):
                    act.wait_ge(s_oT, 1 + b + 1)
                    dst = oT[:, :] if Wo is not None else oT_all[:, bass.ds(b * SEQ, SEQ)]
                    act.activation(dst, turn, ACT.Copy).then_inc(s_oTc, 1)

                def group(b, g, first=False, last=False):
                    q = b * 4 + g
                    for n in range(U2):
                        k, heads = units2[n]
                        act.wait_ge(s_p2, q * U2 + n + 1)
                        act.wait_ge(s_pv, AHEAD + q * 4 + (n - NB) // RU + 1)
                        w = len(queries[k]) * P
                        pair = ps[:, 2 + 2 * (n % 2):4 + 2 * (n % 2), :]
                        src = pair.rearrange("p a (m w) -> p (a m) w", w=W)[:, :, 0:w]
                        act.activation(pt[:, (g * U2 + n) % NB, 0:per2 * w].rearrange("p (h w) -> p h w", w=w), src,
                                       ACT.Exp, scale=SCALE).then_inc(s_exp, 1)
                        if n == 1 and not first:
                            sums_T(q - 1)
                        if n == AT_MAX and not (last and g == 3):
                            rows(q + 1, (g + 1) % 4)
                        if n == AT_SEQ and g == 0 and not first:
                            sequence_T(b - 1)

                rows(0, 0)
                group(0, 0, first=True)
                with act.Fori(0, nb - 1) as b:
                    for g in (1, 2, 3):
                        group(b, g)
                    group(b + 1, 0)
                for g in (1, 2, 3):
                    group(nb - 1, g, last=True)
                sums_T(nb * 4 - 1)
                sequence_T(nb - 1)

            @block.vector
            def _(dve):
                dve.memset(ks[:, 2:4, :, :, :], 0.0).then_inc(s_ones, 1)
                dve.memset(qs[:, :, :, :, :], 0.0).then_inc(s_ones, 1)
                dve.sem_inc(s_oev, 1)
                dve.sem_inc(s_yev, 1)
                def maxima(q, g, n):
                    i, heads = units1[n]
                    dve.wait_ge(s_p1, q * U1 + n + 1)
                    if n == 0 and not isinstance(q, int):
                        dve.wait_ge(s_chain, (q - 2) * CH + CH)
                    hh, prl = heads[0]
                    at = 2 * hh + prl
                    w = len(keys[i]) * P
                    dve.tensor_reduce(nmax[:, g % 2, i, at:at + per1],
                                      ps[:, n % 2, :].rearrange("p (m w) -> p m w", w=W)[:, :, 0:w],
                                      AXX, ALU.max, negate=True).then_inc(s_max, 1)

                def split(q, g):
                    step = Chain(dve, s_chain, q * CH)
                    m, r, part = nmax[:, g % 2, :, :], nrest[:, g % 2, :, :], nparts[:, g % 2, :, :, :]
                    dve.wait_ge(s_max, q * U1 + U1)
                    if not isinstance(q, int) or q >= 2:
                        dve.wait_ge(s_nt, q - 1)
                    step(dve.tensor_copy(part[:, :, :, 0], m))
                    step(dve.tensor_tensor(r, m, part[:, :, :, 0], ALU.subtract))
                    step(dve.tensor_copy(part[:, :, :, 1], r))
                    step(dve.tensor_tensor(part[:, :, :, 2], r, part[:, :, :, 1], ALU.subtract))
                    dve.sem_inc(s_split, 1)

                def sums(b, q, g):
                    dve.wait_ge(s_turn, 1 + q + 1)
                    dve.reciprocal(rden[:, :, :], p_o[:, :, :, HD]).then_inc(s_rd, 1)
                    dve.wait_ge(s_rd, q + 1)
                    if g == 0:
                        dve.wait_ge(s_oT, 1 + b)
                    for hh in range(2):
                        ins = dve.tensor_tensor(
                            oa[:, :, hh, 2 * g * HD:(2 * g + 2) * HD].rearrange("p i (a e) -> p i a e", e=HD),
                            p_o[:, :, 2 * hh:2 * hh + 2, 0:HD],
                            spread(rden[:, :, 2 * hh:2 * hh + 2], HD, 3), ALU.mult)
                    ins.then_inc(s_oev, 1)

                def add_out(b):
                    dve.wait_ge(s_y, b + 1)
                    xs = x[:, bass.ds(b * 4, 4), :]
                    dve.tensor_tensor(xs, xs, turn.rearrange("p (t d) -> p t d", t=4), ALU.add).then_inc(s_yev, 1)

                def group(b, g, first=False, last=False):
                    q = b * 4 + g
                    for n in range(U2):
                        if not (last and g >= 2):
                            for r in range(R):
                                maxima(q + 2, (g + 2) % 4, n * R + r)
                        if n == AT_SUMS and not first:
                            sums(b - 1 if g == 0 else b, q - 1, (g - 1) % 4)
                    if not (last and g >= 2):
                        split(q + 2, (g + 2) % 4)
                    if g == 0 and not first and Wo is not None:
                        add_out(b - 1)

                for g in range(2):
                    for n in range(U1):
                        maxima(g, g, n)
                    split(g, g)
                group(0, 0, first=True)
                with dve.Fori(0, nb - 1) as b:
                    for g in (1, 2, 3):
                        group(b, g)
                    group(b + 1, 0)
                for g in (1, 2, 3):
                    group(nb - 1, g, last=True)
                sums(nb - 1, nb * 4 - 1, 3)
                if Wo is not None:
                    add_out(nb - 1)


def earlier_tiles(nc, C, name, q_feat, k_feat, v_all, inter):
    nt = v_all.shape[1]
    nb = nt // 4
    with Stage(nc, name) as st:
        ps = st.banks()
        qc = st.sb("q_chunk", [P, 2, 3, P])
        kc = st.sb("k_chunk", [P, 2, 3, P])
        own = st.sb("own_head", [P, NH, VC])
        ones = st.sb("ones", [P, NH, VC])
        state = st.sb("state", [P, 2, 3, NH * VC])
        s_own, s_copy, s_kv, s_state, s_qs, s_kept, s_zero = (
            st.sem(n) for n in ("own_ready", "copied", "kv_ready", "state_ready", "qs_ready", "kept", "zeroed"))
        flat = "p h c -> p (h c)"
        with nc.Block() as block:

            @block.gpsimd
            def _(pool):
                step = Chain(pool, s_own)
                step(pool.memset(ones[:, :, :], 1.0))
                step(pool.affine_select(out=own[:, :, :], in_=ones[:, :, :], compare_op=ALU.is_ge, fill=0.0,
                                        base=0, pattern=[[-HD, NH], [0, VC]], channel_multiplier=1))
                step(pool.affine_select(out=own[:, :, :], in_=own[:, :, :], compare_op=ALU.is_ge, fill=0.0,
                                        base=HD - 1, pattern=[[HD, NH], [0, VC]], channel_multiplier=-1))
                with pool.Fori(0, nb // 2) as i:
                    for u in range(2):
                        b = i * 2 + u
                        pool.wait_ge(s_qs, 1 + i * 6)
                        pool.tensor_copy(qc[:, u, :, :], q_feat[:, bass.ds(b * SEQ + P, 3 * P)]
                                         .rearrange("p (c n) -> p c n", c=3)).then_inc(s_copy, 1)
                        pool.tensor_copy(kc[:, u, :, :], k_feat[:, bass.ds(b * SEQ, 3 * P)]
                                         .rearrange("p (c n) -> p c n", c=3)).then_inc(s_copy, 1)

            @block.tensor
            def _(pe):
                pe.sem_inc(s_qs, 1)
                with pe.Fori(0, nb // 2) as i:
                    for u in range(2):
                        b = i * 2 + u
                        pe.wait_ge(s_copy, b * 2 + 2)
                        pe.wait_ge(s_state, 1 + i * 6)
                        for c in range(3):
                            pe.matmul(ps[:, 3 * u + c, 0:NH * VC], kc[:, u, c, :],
                                      v_all[:, bass.ds(b * 4 + c, 1), :, :].rearrange("p a h c -> p (a h c)"),
                                      start=True, stop=True).then_inc(s_kv, 1)
                    for u in range(2):
                        b = i * 2 + u
                        for c in range(3):
                            pe.wait_ge(s_state, 1 + b * 3 + c + 1)
                            pe.wait_ge(s_kept, 1 + i * 2)
                            mm = pe.matmul(ps[:, 6 + u, c * NH * VC:(c + 1) * NH * VC], qc[:, u, c, :],
                                           state[:, u, c, :], start=(c == 0), stop=False, skip_group_check=True)
                            mm.then_inc(s_qs, 1)

            @block.vector
            def _(dve):
                dve.sem_inc(s_state, 1)
                dve.sem_inc(s_kept, 1)
                dve.wait_ge(s_own, 3)
                dve.memset(inter[:, 0:nt:4, :, :].rearrange("p b h c -> p b (h c)"), 0.0).then_inc(s_zero, 1)
                with dve.Fori(0, nb // 2) as i:
                    for u in range(2):
                        for c in range(3):
                            n = i * 6 + 3 * u + c
                            dve.wait_ge(s_kv, n + 1)
                            dve.wait_ge(s_qs, 1 + i * 6)
                            ins = dve.tensor_tensor(state[:, u, c, :], ps[:, 3 * u + c, 0:NH * VC],
                                                    own[:, :, :].rearrange(flat), ALU.mult)
                            if c:
                                ins.then_inc(s_own, 1)
                                dve.wait_ge(s_own, 3 + i * 4 + 2 * u + c)
                                dve.tensor_tensor(state[:, u, c, :], state[:, u, c, :], state[:, u, c - 1, :],
                                                  ALU.add).then_inc(s_state, 1)
                                dve.wait_ge(s_state, 1 + n + 1)
                            else:
                                ins.then_inc(s_state, 1)
                                dve.wait_ge(s_state, 1 + n + 1)
                    for u in range(2):
                        b = i * 2 + u
                        dve.wait_ge(s_qs, 1 + b * 3 + 3)
                        dve.tensor_copy(inter[:, bass.ds(b * 4 + 1, 3), :, :].rearrange("p c h e -> p c (h e)"),
                                        ps[:, 6 + u, 0:3 * NH * VC].rearrange("p (c n) -> p c n", c=3))\
                           .then_inc(s_kept, 1)


def linear_attention(nc, C, name, q_stack, k_stack, v_all, inter, oT_all):
    nb = q_stack.shape[0]
    with Stage(nc, name) as st:
        ps = st.banks()
        qs = st.sb("q_rows", [P, 4, 1, 2, SEQ], BF16)
        ks = st.sb("k_rows", [P, 4, 2, 2, SEQ], BF16)
        s_zero = st.sem("rows_zeroed")
        at = st.sb("weights", [P, 4, 4, P])
        vs = st.sb("values", [P, 4, 4, 4, 32])
        sT = st.sb("sums_T", [P, 2, SEQ])
        tot = st.sb("sums", [P, 4, 4, VC])
        rden = st.sb("one_over_sum", [P, 4, 4])
        oa = st.sb("attended", [P, 4, 2, 8 * HD])
        s_load = [st.sem(f"group{g}_landed") for g in range(4)]
        s_a, s_raw, s_m = st.sem("products_ready"), st.sem("odd_copied"), [st.sem("even_masked"), st.sem("odd_masked")]
        s_pv, s_oev, s_t = st.sem("weights_used"), st.sem("sums_used"), st.sem("dve_chain")
        s_seen, s_v, s_vz = st.sem("pool_has_seen"), st.sem("values_ready"), st.sem("values_zeroed")
        s_sT, s_turn = st.sem("sums_T_ready"), st.sem("sums_turned")
        s_ctx, s_oT, s_oTc = st.sem("attended_ready"), st.sem("attended_turned"), st.sem("attended_T_ready")
        p_oT = [ps[:, 4 + k, :] for k in range(2)]
        turn = ps[:, 6, :]
        p_o = ps[:, 7, :].rearrange("p (i h c) -> p i h c", i=4, h=4)

        def every_group(group, eng):
            group(0, 0)
            group(0, 1)
            with eng.Fori(0, nb - 1) as b:
                group(b, 2)
                group(b, 3)
                group(b + 1, 0)
                group(b + 1, 1)
            group(nb - 1, 2)
            group(nb - 1, 3)

        def is_first(b):
            return isinstance(b, int) and b == 0

        with nc.Block() as block:

            @block.sync
            def _(sp):
                def load(b, g):
                    for stack, dst in ((q_stack, qs), (k_stack, ks)):
                        for hh in range(2):
                            src = stack[bass.ds(b, 1), 8 * hh + 2 * g:8 * hh + 2 * g + 2, :, :]
                            sp.dma_start(dst[64 * hh:64 * hh + ROWS, g, hh if dst is ks else 0, :, :],
                                         src.rearrange("a h r n -> r (a h) n")).then_inc(s_load[g], 16)

                sp.wait_ge(s_zero, 3)
                for g in range(4):
                    load(0, g)
                with sp.Fori(0, nb - 1) as b:
                    for g in range(4):
                        sp.wait_ge(s_a, b * 16 + 4 * g + 4)
                        load(b + 1, g)

            @block.tensor
            def _(pe):
                pe.sem_inc(s_pv, 4)
                pe.sem_inc(s_turn, 2)
                pe.sem_inc(s_oT, 1)

                def products(b, q, g, c):
                    if c == 0:
                        pe.wait_ge(s_load[g], b * 64 + 64)
                    pe.wait_ge(s_m[0] if c % 2 == 0 else s_raw, 1 + q * 2 + c // 2)
                    cols = slice(c * P, (c + 1) * P)
                    for hl in range(4):
                        hh, prl = hl // 2, hl % 2
                        rows = slice(0, 64 + ROWS)
                        mm = pe.matmul(ps[:, 2 * (c % 2) + hh, prl * P:(prl + 1) * P],
                                       ks[rows, g, hh, prl, cols], qs[rows, g, 0, prl, cols],
                                       start=(prl == 0), stop=False, skip_group_check=True)
                    mm.then_inc(s_a, 1)

                def values(q, g, c):
                    pe.wait_ge(s_m[c % 2], 1 + q * 2 + c // 2 + 1)
                    if c == 0:
                        pe.wait_ge(s_v, q * 2 + 2)
                        pe.wait_ge(s_sT, 1 + q)
                    for hl in range(4):
                        mm = pe.matmul(p_oT[g % 2][32 * hl:32 * hl + 32, c * P:(c + 1) * P], vs[:, g, c, hl, :],
                                       at[:, c, hl, :], start=(c == 0), stop=False, skip_group_check=True)
                    mm.then_inc(s_pv, 1)

                def turn_sums(q, g):
                    pe.wait_ge(s_sT, 2 + q + 1)
                    pe.wait_ge(s_oev, 1 + q)
                    for i in range(4):
                        mm = pe.transpose(ps[:, 7, i * P:(i + 1) * P], sT[:, g % 2, i * P:(i + 1) * P],
                                          C["ident"][:, :])
                    mm.then_inc(s_turn, 1)

                def turn_sequence(b):
                    pe.wait_ge(s_ctx, b * 4 + 4)
                    pe.wait_ge(s_oTc, 1 + b)
                    for i in range(4):
                        mm = pe.transpose(turn[:, i * P:(i + 1) * P], oa[:, i, :, :].rearrange("p a c -> p (a c)"),
                                          C["ident"][:, :])
                    mm.then_inc(s_oT, 1)

                def group(b, g):
                    q = b * 4 + g
                    first = is_first(b) and g == 0
                    for c in range(4):
                        products(b, q, g, c)
                        if c >= 2:
                            values(q, g, c - 2)
                        elif not first:
                            values(q - 1, (g - 1) % 4, c + 2)
                        if c == 0 and g == 1 and not is_first(b):
                            turn_sequence(b - 1)
                        if c == 3 and not first:
                            turn_sums(q - 1, (g - 1) % 4)

                every_group(group, pe)
                last = nb * 4 - 1
                values(last, 3, 2)
                values(last, 3, 3)
                turn_sums(last, 3)
                turn_sequence(nb - 1)

            @block.scalar
            def _(act):
                act.sem_inc(s_raw, 1)
                act.sem_inc(s_oTc, 1)
                act.sem_inc(s_sT, 2)

                def sums_T(q, g):
                    act.wait_ge(s_pv, 4 + q * 4 + 4)
                    act.wait_ge(s_turn, 1 + q)
                    act.activation(sT[:, g % 2, :], p_oT[g % 2], ACT.Copy).then_inc(s_sT, 1)

                def sequence_T(b):
                    act.wait_ge(s_oT, 1 + b + 1)
                    act.activation(oT_all[:, bass.ds(b * SEQ, SEQ)], turn, ACT.Copy).then_inc(s_oTc, 1)

                def group(b, g):
                    q = b * 4 + g
                    for c in (1, 3):
                        act.wait_ge(s_a, q * 4 + c + 1)
                        act.wait_ge(s_pv, 4 + q * 4 + c - 3)
                        act.activation(at[:, c, :, :].rearrange("p (a h) c -> p a (h c)", a=2), ps[:, 2:4, 0:2 * P],
                                       ACT.Copy).then_inc(s_raw, 1)
                        if c == 1 and not (is_first(b) and g == 0):
                            sums_T(q - 1, (g - 1) % 4)
                        if c == 1 and g == 1 and not is_first(b):
                            sequence_T(b - 1)

                every_group(group, act)
                sums_T(nb * 4 - 1, 3)
                sequence_T(nb - 1)

            @block.gpsimd
            def _(pool):
                pool.sem_inc(s_m[1], 1)
                pool.memset(ks[:, 0:2, :, :, :], 0.0).then_inc(s_zero, 1)
                pool.memset(vs[:, :, :, :, :], 0.0).then_inc(s_vz, 1)

                def copy_values(b, g):
                    for hh in range(2):
                        pool.tensor_copy(vs[:, g, :, 2 * hh:2 * hh + 2, 0:VC],
                                         v_all[:, bass.ds(b * 4, 4), 8 * hh + 2 * g:8 * hh + 2 * g + 2, :])\
                            .then_inc(s_v, 1)

                def group(b, g):
                    q = b * 4 + g
                    if not (isinstance(b, int) and b == nb - 1 and g >= 2):
                        if not is_first(b) or g >= 2:
                            pool.wait_ge(s_pv, q * 4)
                            pool.sem_inc(s_seen, 1)
                        copy_values(b + (1 if g >= 2 else 0), (g + 2) % 4)
                    for c in (1, 3):
                        pool.wait_ge(s_raw, 1 + q * 2 + c // 2 + 1)
                        pool.sem_inc(s_seen, 1)
                        pool.affine_select(out=at[:, c, :, :], in_=at[:, c, :, :], compare_op=ALU.is_ge,
                                           fill=0.0, base=0, pattern=[[0, 4], [1, P]], channel_multiplier=-1)\
                            .then_inc(s_m[1], 1)

                pool.wait_ge(s_vz, 1)
                copy_values(0, 0)
                copy_values(0, 1)
                every_group(group, pool)

            @block.vector
            def _(dve):
                dve.memset(ks[:, 2:4, :, :, :], 0.0).then_inc(s_zero, 1)
                dve.memset(qs[:, :, :, :, :], 0.0).then_inc(s_zero, 1)
                dve.sem_inc(s_oev, 1)
                dve.sem_inc(s_m[0], 1)
                CH = 3

                def sums(b, q, g):
                    step = Chain(dve, s_t, q * CH)
                    dve.wait_ge(s_turn, 2 + q + 1)
                    if g == 0:
                        dve.wait_ge(s_oT, 1 + b)
                    for hh in range(2):
                        ins = dve.tensor_tensor(
                            tot[:, :, 2 * hh:2 * hh + 2, :],
                            p_o[:, :, 2 * hh:2 * hh + 2, 0:VC],
                            inter[:, bass.ds(b * 4, 4), 8 * hh + 2 * g:8 * hh + 2 * g + 2, :], ALU.add)
                        if hh:
                            ins.then_inc(s_oev, 1)
                    dve.wait_ge(s_oev, 1 + q + 1)
                    step(dve.tensor_scalar(rden[:, :, :], tot[:, :, :, HD], 1e-6, None, ALU.add))
                    step(dve.reciprocal(rden[:, :, :], rden[:, :, :]))
                    for hh in range(2):
                        ins = dve.tensor_tensor(
                            oa[:, :, hh, 2 * g * HD:(2 * g + 2) * HD].rearrange("p i (a e) -> p i a e", e=HD),
                            tot[:, :, 2 * hh:2 * hh + 2, 0:HD],
                            spread(rden[:, :, 2 * hh:2 * hh + 2], HD, 3), ALU.mult)
                    step(ins)
                    dve.sem_inc(s_ctx, 1)

                def group(b, g):
                    q = b * 4 + g
                    for c in (0, 2):
                        dve.wait_ge(s_a, q * 4 + c + 1)
                        dve.wait_ge(s_pv, 4 + q * 4 + c - 3)
                        dve.tensor_tensor(at[:, c, :, :].rearrange("p (a h) c -> p a h c", a=2),
                                          ps[:, 0:2, 0:2 * P].rearrange("p a (h c) -> p a h c", h=2),
                                          spread(spread(C["upto_bf"][:, :], 2, 1), 2, 1), ALU.mult)\
                           .then_inc(s_m[0], 1)
                    if not (is_first(b) and g == 0):
                        sums(b - 1 if g == 0 else b, q - 1, (g - 1) % 4)

                every_group(group, dve)
                sums(nb - 1, nb * 4 - 1, 3)


def mix(nc, C, name, x_in, oT_a, oT_s, Wp, Wos, Wo, bias_col, bo_at):
    nch = x_in.shape[1] // 4
    with Stage(nc, name) as st:
        ps = st.banks()
        both = st.sb("both", [P, 2, SEQ])
        s_b, s_bev, s_y, s_yev = st.sem("both_ready"), st.sem("both_kept"), st.sem("out_ready"), st.sem("out_added")
        with nc.Block() as block:

            @block.tensor
            def _(pe):
                pe.sem_inc(s_y, 2)
                with pe.Fori(0, nch // 2) as i:
                    for u in range(2):
                        c = i * 2 + u
                        pe.wait_ge(s_bev, c + 1)
                        pe.matmul(ps[:, u, :], Wp, oT_a[:, bass.ds(c * SEQ, SEQ)], start=True, stop=False)
                        pe.matmul(ps[:, u, :], Wos, oT_s[:, bass.ds(c * SEQ, SEQ)], start=False, stop=True)\
                          .then_inc(s_b, 1)
                    for u in range(2):
                        c = i * 2 + u
                        pe.wait_ge(s_bev, 2 + c + 1)
                        pe.wait_ge(s_yev, c + 1)
                        for k in range(4):
                            o = ps[:, 2 + u, k * P:(k + 1) * P]
                            pe.matmul(o, C["ones_bf"][0:3, :], C["bias_rows"][:, bo_at:bo_at + P],
                                      start=(k == 0), stop=False, skip_group_check=True)
                            mm = pe.matmul(o, both[:, u, k * P:(k + 1) * P], Wo, start=False, stop=False,
                                           skip_group_check=True)
                        mm.then_inc(s_y, 1)

            @block.scalar
            def _(act):
                act.sem_inc(s_bev, 2)
                with act.Fori(0, nch // 2) as i:
                    for u in range(2):
                        c = i * 2 + u
                        act.wait_ge(s_b, c + 1)
                        act.wait_ge(s_y, c + 1)
                        act.activation(both[:, u, :], ps[:, u, :], ACT.Identity, bias=bias_col).then_inc(s_bev, 1)

            @block.vector
            def _(dve):
                dve.sem_inc(s_yev, 2)
                with dve.Fori(0, nch // 2) as i:
                    for u in range(2):
                        c = i * 2 + u
                        dve.wait_ge(s_y, 2 + c + 1)
                        xs = x_in[:, bass.ds(c * 4, 4), :]
                        dve.tensor_tensor(xs, xs, ps[:, 2 + u, :].rearrange("p (t d) -> p t d", t=4), ALU.add)\
                           .then_inc(s_yev, 1)


def dense_mlp(nc, C, name, x, x1, hT_all, W1, b1, W2, b2_at):
    nch = x.shape[1] // 4
    NC = W1.shape[1] // P
    with Stage(nc, name) as st:
        ps = st.banks()
        g = st.sb("gelu", [P, 2, NC, SEQ])
        s_h, s_g, s_y, s_x1, s_yev = (st.sem(n) for n in ("hidden_ready", "gelu_ready", "out_ready", "x1_added",
                                                          "out_added"))
        with nc.Block() as block:

            @block.tensor
            def _(pe):
                pe.sem_inc(s_y, 2)
                def first(i, u):
                    n = i * 2 + u
                    for c in range(NC):
                        pe.wait_ge(s_g, n * NC + c + 1)
                        pe.matmul(ps[:, c, :], W1[:, c * P:(c + 1) * P], hT_all[:, bass.ds(n * SEQ, SEQ)],
                                  start=True, stop=True).then_inc(s_h, 1)

                def second(i, u):
                    n = i * 2 + u
                    pe.wait_ge(s_g, NC + (n + 1) * NC)
                    pe.wait_ge(s_yev, n + 1)
                    for k in range(4):
                        o = ps[:, 4 + u, k * P:(k + 1) * P]
                        pe.matmul(o, C["ones_bf"][0:3, :], C["bias_rows"][:, b2_at:b2_at + P],
                                  start=(k == 0), stop=False, skip_group_check=True)
                        for c in range(NC):
                            mm = pe.matmul(o, g[:, u, c, k * P:(k + 1) * P], W2[:, c, :], start=False, stop=False,
                                           skip_group_check=True)
                    mm.then_inc(s_y, 1)

                with pe.Fori(0, nch // 2) as i:
                    first(i, 0)
                    first(i, 1)
                    second(i, 0)
                    second(i, 1)

            @block.scalar
            def _(act):
                act.sem_inc(s_g, NC)
                with act.Fori(0, nch // 2) as i:
                    for u in range(2):
                        for c in range(NC):
                            act.wait_ge(s_h, i * 2 * NC + u * NC + c + 1)
                            act.wait_ge(s_y, i * 2 + u + 1)
                            act.activation(g[:, u, c, :], ps[:, c, :], ACT.Gelu, bias=b1[:, c:c + 1]).then_inc(s_g, 1)

            @block.gpsimd
            def _(pool):
                with pool.Fori(0, nch) as i:
                    xs = x[:, bass.ds(i * 4, 4), :]
                    pool.tensor_tensor(xs, xs, x1[:, bass.ds(i * 4, 4), :], ALU.add).then_inc(s_x1, 1)

            @block.vector
            def _(dve):
                dve.sem_inc(s_yev, 2)
                with dve.Fori(0, nch // 2) as i:
                    for u in range(2):
                        c = i * 2 + u
                        dve.wait_ge(s_y, 2 + c + 1)
                        dve.wait_ge(s_x1, c + 1)
                        xs = x[:, bass.ds(c * 4, 4), :]
                        dve.tensor_tensor(xs, xs, ps[:, 4 + u, :].rearrange("p (t d) -> p t d", t=4), ALU.add)\
                           .then_inc(s_yev, 1)


def build(nc, a, out, upto="all"):
    nt = 32
    row_biases = [(a["be"], 1024), (a["b2"], 1024), (a["bva"], 128), (a["bks"], 128), (a["bvs"], 128),
                  (a["bo"], 128), (a["b2m"], 128)]
    at, BIAS_AT = 0, {}
    for nm, (_, n) in zip(("be", "b2", "va", "ks", "vs", "bo", "b2m"), row_biases):
        BIAS_AT[nm] = at
        at += n
    with Stage(nc, "all") as st:
        C = {
            "ident": st.sb("ident", [P, P]), "ident_bf": st.sb("ident_bf", [P, P], BF16),
            "ones_bf": st.sb("ones_bf", [P, P], BF16), "zero_bf": st.sb("zero_bf", [P, P], BF16),
            "upto_bf": st.sb("upto_bf", [P, P], BF16),
            "col_ge": st.sb("col_ge", [P, 4, P], BF16), "col_gt": st.sb("col_gt", [P, 4, P], BF16),
            "col_le": st.sb("col_le", [P, 4, P], BF16), "col_lt": st.sb("col_lt", [P, 4, P], BF16),
            "rank": st.sb("rank", [P, 8]),
            "bit": st.sb("bit", [P, BITS, 8]), "bit_i": st.sb("bit_int", [P, BITS, 8], U32),
            "bias_rows": st.sb("bias_rows", [3, at], BF16),
        }
        x = st.sb("x", [P, nt, D])
        logits = st.sb("logits", [P, nt, 8])
        wg, bg, wr = st.sb("wg", [P, 8]), st.sb("bg", [P, 8]), st.sb("wr", [P, 8])
        xn_rows = nc.dram_tensor("xn_rows", [nt * P, D], F32, kind="Internal").ap()
        acc_rows = nc.dram_tensor("acc_rows", [nt * P, D], F32, kind="Internal").ap()
        make_constants(nc, C, row_biases)
        with Stage(nc, "load") as ld:
            s = ld.sem("landed")
            with nc.Block() as block:
                @block.sync
                def _(sp):
                    sp.dma_start(x[:, :, :], a["x"].rearrange("b (t p) d -> p (b t) d", p=P)).then_inc(s, 16)
                    sp.dma_start(wg[:, :], a["Wg"]).then_inc(s, 16)
                    sp.dma_start(wr[:, :], a["Wr"]).then_inc(s, 16)
                    sp.dma_start(bg[:, :], a["bg"].broadcast_to([P, 8])).then_inc(s, 16)
                    sp.wait_ge(s, 64)

        def moe(name):
            with Stage(nc, name + "T") as t:
                xT = t.sb("xT_all", [P, nt * P])
                norm_stage(nc, C, name + "n", x, xT_all=xT, router=wg[:, :], logits=logits, router_bias=bg)
                linear_experts(nc, C, name + "e", x, xT, logits, a["We"], BIAS_AT["be"])

        def ffn(name):
            with Stage(nc, name + "S") as t:
                slot_id = t.sb("slot_id", [P, 8, 8], U32)
                slot_gate = t.sb("slot_gate", [P, 8, 8])
                b1col = t.sb("b1col", [P, 8, 4])
                s = t.sem("b1_landed")
                with nc.Block() as block:
                    @block.sync
                    def _(sp):
                        sp.dma_start(b1col[:, :, :], a["c_fb1"]).then_inc(s, 16)
                        sp.wait_ge(s, 16)
                norm_stage(nc, C, name + "n", x, router=wr[:, :], logits=logits, norm_to_dram=xn_rows,
                           x_to_dram=acc_rows)
                choose_tokens(nc, C, name + "c", logits, 1024, slot_id, slot_gate)
                expert_mlps(nc, C, name + "m", x, xn_rows, acc_rows, slot_id, slot_gate, a["F1"], b1col, a["F2"],
                            BIAS_AT["b2"])

        q_stack = nc.dram_tensor("q_stack", [8, NH, ROWS, SEQ], BF16, kind="Internal").ap()
        k_stack = nc.dram_tensor("k_stack", [8, NH, ROWS, SEQ], BF16, kind="Internal").ap()

        def load_all(name, pairs):
            with Stage(nc, name) as ld:
                s = ld.sem("landed")
                with nc.Block() as block:
                    @block.sync
                    def _(sp):
                        for dst, src in pairs:
                            sp.dma_start(dst, src).then_inc(s, 16)
                        sp.wait_ge(s, 16 * len(pairs))

        def attn0():
            with Stage(nc, "att") as t:
                w = [t.sb(n, [P, P]) for n in ("wq", "wk", "wv", "wo")]
                load_all("attl", [(d[:, :], a[n]) for d, n in zip(w, ("Wq", "Wk", "Wv", "WoT"))])
                v_all = t.sb("v_all", [P, nt, NH, VC])
                with Stage(nc, "attx") as tx:
                    xT = tx.sb("xT_all", [P, nt * P])
                    norm_stage(nc, C, "attn", x, xT_all=xT)
                    project(nc, C, "attp", xT, w[0][:, :], w[1][:, :], w[2][:, :], q_stack, k_stack, v_all)
                window_attention(nc, C, "attw", q_stack, k_stack, v_all, False, x=x, Wo=w[3][:, :])

        def attn1():
            with Stage(nc, "two") as t:
                x_in = t.sb("x_in", [P, nt, D])
                oT_a, oT_s = t.sb("oT_a", [P, nt * P]), None
                wa, ws = t.sb("wqkv_a", [P, 3 * D]), t.sb("wqkv_s", [P, 3 * D])
                wp, wos, wo = (t.sb(n, [P, D]) for n in ("wp", "wos", "wo"))
                cols = {n: t.sb(n, [P, m]) for n, m in (("g1", 1), ("b1", 1), ("bqkv_a", 3), ("bp_a", 1),
                                                        ("bqkv_s", 3), ("bo_s", 1), ("gm", 1), ("bm", 1), ("b1m", 4))}
                load_all("twol", [(wa[:, :], a["AWqkv_a"]), (ws[:, :], a["AWqkv_s"]), (wp[:, :], a["AWp_a"]),
                                  (wos[:, :], a["AWo_s"]), (wo[:, :], a["AWo"])]
                         + [(d[:, :], a["c_" + n]) for n, d in cols.items()])
                with Stage(nc, "twob") as tb:
                    s = tb.sem("biases")
                    with nc.Block() as block:
                        @block.vector
                        def _(dve):
                            dve.tensor_tensor(cols["bp_a"][:, :], cols["bp_a"][:, :], cols["bo_s"][:, :],
                                              ALU.add).then_inc(s, 1)
                            dve.tensor_scalar(cols["bqkv_s"][:, 0:1], cols["bqkv_s"][:, 0:1], HD ** -0.5, None,
                                              ALU.mult).then_inc(s, 1)
                norm_stage(nc, C, "two1", x, keep_norm=x_in)
                with Stage(nc, "twox") as tx:
                    xT = tx.sb("xT_all", [P, nt * P])
                    norm_stage(nc, C, "two2", x_in, xT_all=xT, gain=cols["g1"][:, :], shift=cols["b1"][:, :])
                    with Stage(nc, "twow") as tw:
                        v_all = tw.sb("v_all", [P, nt, NH, VC])
                        project(nc, C, "two3", xT, wa[:, 0:D], wa[:, D:2 * D], wa[:, 2 * D:3 * D], q_stack, k_stack,
                                v_all, bq=cols["bqkv_a"][:, 0:1], bk=cols["bqkv_a"][:, 1:2], v_bias=BIAS_AT["va"])
                        window_attention(nc, C, "two4", q_stack, k_stack, v_all, True, oT_all=oT_a)
                    with Stage(nc, "twos") as ts:
                        v_all = ts.sb("v_all", [P, nt, NH, VC])
                        with Stage(nc, "twoq") as tq:
                            q_feat, k_feat = tq.sb("q_feat", [P, nt * P]), tq.sb("k_feat", [P, nt * P])
                            project(nc, C, "two5", xT, ws[:, 0:D], ws[:, D:2 * D], ws[:, 2 * D:3 * D], q_stack,
                                    k_stack, v_all, bq=cols["bqkv_s"][:, 0:1], bk=cols["bqkv_s"][:, 1:2],
                                    v_bias=BIAS_AT["vs"],
                                    linear=dict(scale=HD ** -0.5, q=q_feat, k=k_feat, k_bias=BIAS_AT["ks"]))
                            inter = tq.sb("inter", [P, nt, NH, VC])
                            earlier_tiles(nc, C, "two6", q_feat, k_feat, v_all, inter)
                            linear_attention(nc, C, "two7", q_stack, k_stack, v_all, inter, xT)
                    mix(nc, C, "two8", x_in, oT_a, xT, wp[:, :], wos[:, :], wo[:, :], cols["bp_a"][:, :],
                        BIAS_AT["bo"])
                    w1, w2 = tx.sb("w1", [P, 4 * D]), tx.sb("w2", [P, 4, D])
                    load_all("two9", [(w1[:, :], a["W1m"]), (w2[:, :, :], a["W2m"].rearrange("(c f) d -> f c d", f=P))])
                    norm_stage(nc, C, "twoa", x_in, xT_all=xT, gain=cols["gm"][:, :], shift=cols["bm"][:, :])
                    dense_mlp(nc, C, "twoc", x, x_in, xT, w1, cols["b1m"], w2, BIAS_AT["b2m"])

        if upto == "all":
            moe("moe0")
            attn0()
            moe("moe1")
            ffn("ffn0")
            attn1()
            ffn("ffn1")
        if "B" in upto:
            attn0()
        if "E" in upto:
            attn1()
        if "A" in upto:
            moe("moe0")
        if "D" in upto:
            ffn("ffn0")
        with Stage(nc, "store") as so:
            s = so.sem("stored")
            with nc.Block() as block:
                @block.sync
                def _(sp):
                    sp.dma_start(out.rearrange("b (t p) d -> p (b t) d", p=P), x[:, :, :]).then_inc(s, 16)
                    sp.wait_ge(s, 16)


def layout(v):
    import numpy as np

    def rows(a):
        return a.reshape(1, -1)

    def columns(a):
        return a.reshape(-1, P).T

    d = {
        "x": v["L0_attn_x"], "Wq": v["L0_attn_Wq"].T, "Wk": v["L0_attn_Wk"].T, "Wv": v["L0_attn_Wv"].T,
        "WoT": v["L0_attn_Wo"].T, "Wg": v["L0_ffn_Wg"], "bg": rows(v["L0_ffn_bg"]),
        "We": v["L0_ffn_We"].transpose(2, 0, 1).reshape(D, -1), "be": rows(v["L0_ffn_be"]),
        "Wr": v["L1_ffn_Wr"], "b2": rows(v["L1_ffn_b2"]),
        "bva": rows(v["L1_attn_bqkv_a"][2 * D:]), "bks": rows(v["L1_attn_bqkv_s"][D:2 * D]),
        "bvs": rows(v["L1_attn_bqkv_s"][2 * D:]), "bo": rows(v["L1_attn_bo"]), "b2m": rows(v["L1_attn_b2m"]),
        "AWqkv_a": v["L1_attn_Wqkv_a"], "AWp_a": v["L1_attn_Wp_a"], "AWqkv_s": v["L1_attn_Wqkv_s"],
        "AWo_s": v["L1_attn_Wo_s"], "AWo": v["L1_attn_Wo"], "W1m": v["L1_attn_W1"], "W2m": v["L1_attn_W2"],
        "F1": v["L1_ffn_W1"], "F2": v["L1_ffn_W2"],
        "c_fb1": v["L1_ffn_b1"].reshape(8, 4, P).transpose(2, 0, 1),
    }
    for n in ("g1", "b1", "bqkv_a", "bp_a", "bqkv_s", "bo_s", "gm", "bm", "b1m"):
        d["c_" + n] = columns(v["L1_attn_" + n])
    return {n: np.ascontiguousarray(a) for n, a in d.items()}


def kernel(**inputs):
    import numpy as np
    import concourse.bacc as bacc
    from concourse.bass_utils import run_bass_kernel_spmd

    nc = bacc.Bacc("TRN2", target_bir_lowering=False, num_devices=1)
    arrays = layout({n: np.asarray(a) for n, a in inputs.items()})
    aps = {n: nc.dram_tensor(f"in_{n}", a.shape, mybir.dt.from_np(a.dtype), kind="ExternalInput").ap()
           for n, a in arrays.items()}
    out = nc.dram_tensor("out_0_dram", inputs["L0_attn_x"].shape, F32, kind="ExternalOutput").ap()
    build(nc, aps, out)
    r = run_bass_kernel_spmd(nc, [{f"in_{n}": a for n, a in arrays.items()}], core_ids=[0])
    return r.results[0]["out_0_dram"]
```
